# Optimizing a Trainium2 kernel written in Bass

```python
import numpy as np
import jax
import jax.numpy as jnp

def _softmax(x, axis=-1):
    return jax.nn.softmax(x, axis=axis)

def _gelu(x):
    return jax.nn.gelu(x, approximate=True)

def _silu(x):
    return jax.nn.silu(x)

def _sigmoid(x):
    return jax.nn.sigmoid(x)

def _layernorm(x, axis=-1, eps=1e-05):
    m = jnp.mean(x, axis=axis, keepdims=True)
    v = jnp.var(x, axis=axis, keepdims=True)
    return (x - m) / jnp.sqrt(v + eps)

def _scatter_add(tgt, idx, src, axis=0):
    return tgt.at[idx].add(src)

def _segment_sum(src, seg, n):
    return jax.ops.segment_sum(src, seg, n)
kernel_name = 'mk_prb_d2_jaxref_r8_f41578'

def setup_inputs(seed: int=0):
    np.random.seed(seed)
    _w = jnp.asarray

    def _L0_attn_setup():
        import jax, jax.numpy as jnp
        import numpy as np
        HEADS = 16
        key = jax.random.key(seed)
        ks = jax.random.split(key, 5)
        B, T, D = (2, 256, 256)
        s = 0.02
        return {'x': jax.random.normal(ks[0], (B, T, D), dtype=jnp.float32), 'Wq': jax.random.normal(ks[1], (D, D), dtype=jnp.float32) * s, 'Wk': jax.random.normal(ks[2], (D, D), dtype=jnp.float32) * s, 'Wv': jax.random.normal(ks[3], (D, D), dtype=jnp.float32) * s, 'Wo': jax.random.normal(ks[4], (D, D), dtype=jnp.float32) * s}
    _L0_attn_in = _L0_attn_setup()

    def _L0_ffn_setup():
        import jax, jax.numpy as jnp
        import numpy as np
        NUM_EXPERTS = 64
        TOP_K = 8
        HIDDEN = 256
        FFN = 96
        BATCH, SEQ = (1, 256)
        CAP_FACTOR = 2

        def _moe_forward(hidden_states, gate_w, w_gate, w_up, w_down):
            B, S, D = hidden_states.shape
            E = gate_w.shape[0]
            x = hidden_states.reshape(-1, D)
            N = x.shape[0]
            P = N * TOP_K
            C = CAP_FACTOR * P // E
            logits = x @ gate_w.T
            probs = jax.nn.softmax(logits, axis=-1)
            scores, idx = jax.lax.top_k(probs, TOP_K)
            flat_e = idx.reshape(-1)
            order = jnp.argsort(flat_e)
            e_sorted = flat_e[order]
            tok_sorted = order // TOP_K
            s_sorted = scores.reshape(-1)[order]
            counts = jnp.bincount(e_sorted, length=E)
            starts = jnp.cumsum(counts) - counts
            pos = jnp.arange(P) - starts[e_sorted]
            valid = pos < C
            safe_pos = jnp.minimum(pos, C - 1)
            xbuf = jnp.zeros((E, C, D), dtype=x.dtype).at[e_sorted, pos].set(x[tok_sorted], mode='drop')
            g = jnp.einsum('ecd,efd->ecf', xbuf, w_gate)
            u = jnp.einsum('ecd,efd->ecf', xbuf, w_up)
            y = jnp.einsum('ecf,edf->ecd', jax.nn.silu(g) * u, w_down)
            y_pair = y[e_sorted, safe_pos] * (s_sorted * valid)[:, None]
            out = jnp.zeros((N, D), dtype=x.dtype).at[tok_sorted].add(y_pair)
            return out.reshape(B, S, D)
        key = jax.random.key(seed)
        k1, k2, k3, k4, k5 = jax.random.split(key, 5)
        hidden_states = jax.random.normal(k1, (BATCH, SEQ, HIDDEN), dtype=jnp.float32)
        gate_w = jax.random.normal(k2, (NUM_EXPERTS, HIDDEN), dtype=jnp.float32) * 0.02
        w_gate = jax.random.normal(k3, (NUM_EXPERTS, FFN, HIDDEN), dtype=jnp.float32) * 0.02
        w_up = jax.random.normal(k4, (NUM_EXPERTS, FFN, HIDDEN), dtype=jnp.float32) * 0.02
        w_down = jax.random.normal(k5, (NUM_EXPERTS, HIDDEN, FFN), dtype=jnp.float32) * 0.02
        return {'hidden_states': hidden_states, 'gate_w': gate_w, 'w_gate': w_gate, 'w_up': w_up, 'w_down': w_down}
    _L0_ffn_in = _L0_ffn_setup()

    def _L1_attn_setup():
        import math
        import jax, jax.numpy as jnp
        import numpy as np
        D_MODEL = 256
        NUM_HEADS = 16
        HEAD_DIM = D_MODEL // NUM_HEADS
        B, T = (2, 256)
        key = jax.random.key(seed)
        ks = jax.random.split(key, 5)
        s = 1.0 / math.sqrt(D_MODEL)
        return {'x': jax.random.normal(ks[0], (B, T, D_MODEL), dtype=jnp.float32), 'Wq': jax.random.normal(ks[1], (D_MODEL, D_MODEL), dtype=jnp.float32) * s, 'Wk': jax.random.normal(ks[2], (D_MODEL, D_MODEL), dtype=jnp.float32) * s, 'Wv': jax.random.normal(ks[3], (D_MODEL, D_MODEL), dtype=jnp.float32) * s, 'Wo': jax.random.normal(ks[4], (D_MODEL, D_MODEL), dtype=jnp.float32) * s}
    _L1_attn_in = _L1_attn_setup()

    def _L1_ffn_setup():
        import jax, jax.numpy as jnp
        import numpy as np
        DIM_IN = 256
        DIM_HIDDEN = 1024
        key = jax.random.key(seed)
        k_x, k_g, k_u, k_d = jax.random.split(key, 4)
        s_in = 1.0 / np.sqrt(DIM_IN)
        s_hid = 1.0 / np.sqrt(DIM_HIDDEN)
        x = jax.random.normal(k_x, (4, 256, DIM_IN), dtype=jnp.float32)
        w_gate = jax.random.uniform(k_g, (DIM_HIDDEN, DIM_IN), jnp.float32, -s_in, s_in)
        w_up = jax.random.uniform(k_u, (DIM_HIDDEN, DIM_IN), jnp.float32, -s_in, s_in)
        w_down = jax.random.uniform(k_d, (DIM_IN, DIM_HIDDEN), jnp.float32, -s_hid, s_hid)
        return {'x': x, 'w_gate': w_gate, 'w_up': w_up, 'w_down': w_down}
    _L1_ffn_in = _L1_ffn_setup()
    _d = {'L0_attn_x': _L0_attn_in['x'], 'L0_attn_Wq': _L0_attn_in['Wq'], 'L0_attn_Wk': _L0_attn_in['Wk'], 'L0_attn_Wv': _L0_attn_in['Wv'], 'L0_attn_Wo': _L0_attn_in['Wo'], 'L0_ffn_gate_w': _L0_ffn_in['gate_w'], 'L0_ffn_w_gate': _L0_ffn_in['w_gate'], 'L0_ffn_w_up': _L0_ffn_in['w_up'], 'L0_ffn_w_down': _L0_ffn_in['w_down'], 'L1_attn_Wq': _L1_attn_in['Wq'], 'L1_attn_Wk': _L1_attn_in['Wk'], 'L1_attn_Wv': _L1_attn_in['Wv'], 'L1_attn_Wo': _L1_attn_in['Wo'], 'L1_ffn_w_gate': _L1_ffn_in['w_gate'], 'L1_ffn_w_up': _L1_ffn_in['w_up'], 'L1_ffn_w_down': _L1_ffn_in['w_down']}
    _x0 = _d['L0_attn_x']
    _d['L0_attn_x'] = jax.random.normal(jax.random.fold_in(jax.random.key(seed), 1), (4, 256, 256), dtype=_x0.dtype)
    del _x0
    return _d

def reference(L0_attn_x, L0_attn_Wq, L0_attn_Wk, L0_attn_Wv, L0_attn_Wo, L0_ffn_gate_w, L0_ffn_w_gate, L0_ffn_w_up, L0_ffn_w_down, L1_attn_Wq, L1_attn_Wk, L1_attn_Wv, L1_attn_Wo, L1_ffn_w_gate, L1_ffn_w_up, L1_ffn_w_down):

    def _L0_attn_ref(x, Wq, Wk, Wv, Wo):
        import jax, jax.numpy as jnp
        import numpy as np
        HEADS = 16
        B, T, _ = x.shape
        H = HEADS
        Dh = Wq.shape[1] // H
        q = (x @ Wq).reshape(B, T, H, Dh)
        k = (x @ Wk).reshape(B, T, H, Dh)
        v = (x @ Wv).reshape(B, T, H, Dh)
        scores = jnp.einsum('bthd,bshd->bhts', q, k)
        mask = jnp.tril(jnp.ones((T, T), dtype=scores.dtype))
        scores = scores * mask
        attn = jax.nn.softmax(scores / T ** 0.5, axis=-1)
        out = jnp.einsum('bhts,bshd->bthd', attn, v).reshape(B, T, H * Dh)
        return out @ Wo

    def _L0_ffn_ref(hidden_states, gate_w, w_gate, w_up, w_down):
        import jax, jax.numpy as jnp
        import numpy as np
        NUM_EXPERTS = 64
        TOP_K = 8
        HIDDEN = 256
        FFN = 96
        BATCH, SEQ = (1, 256)
        CAP_FACTOR = 2

        def _moe_forward(hidden_states, gate_w, w_gate, w_up, w_down):
            B, S, D = hidden_states.shape
            E = gate_w.shape[0]
            x = hidden_states.reshape(-1, D)
            N = x.shape[0]
            P = N * TOP_K
            C = CAP_FACTOR * P // E
            logits = x @ gate_w.T
            probs = jax.nn.softmax(logits, axis=-1)
            scores, idx = jax.lax.top_k(probs, TOP_K)
            flat_e = idx.reshape(-1)
            order = jnp.argsort(flat_e)
            e_sorted = flat_e[order]
            tok_sorted = order // TOP_K
            s_sorted = scores.reshape(-1)[order]
            counts = jnp.bincount(e_sorted, length=E)
            starts = jnp.cumsum(counts) - counts
            pos = jnp.arange(P) - starts[e_sorted]
            valid = pos < C
            safe_pos = jnp.minimum(pos, C - 1)
            xbuf = jnp.zeros((E, C, D), dtype=x.dtype).at[e_sorted, pos].set(x[tok_sorted], mode='drop')
            g = jnp.einsum('ecd,efd->ecf', xbuf, w_gate)
            u = jnp.einsum('ecd,efd->ecf', xbuf, w_up)
            y = jnp.einsum('ecf,edf->ecd', jax.nn.silu(g) * u, w_down)
            y_pair = y[e_sorted, safe_pos] * (s_sorted * valid)[:, None]
            out = jnp.zeros((N, D), dtype=x.dtype).at[tok_sorted].add(y_pair)
            return out.reshape(B, S, D)
        return _moe_forward(hidden_states, gate_w, w_gate, w_up, w_down)

    def _L1_attn_ref(x, Wq, Wk, Wv, Wo):
        import math
        import jax, jax.numpy as jnp
        import numpy as np
        D_MODEL = 256
        NUM_HEADS = 16
        HEAD_DIM = D_MODEL // NUM_HEADS
        B, T = (2, 256)
        Bx, Tx, C = x.shape
        H, D = (NUM_HEADS, HEAD_DIM)
        q = (x @ Wq.T).reshape(Bx, Tx, H, D).transpose(0, 2, 1, 3)
        k = (x @ Wk.T).reshape(Bx, Tx, H, D).transpose(0, 2, 1, 3)
        v = (x @ Wv.T).reshape(Bx, Tx, H, D).transpose(0, 2, 1, 3)
        scale = math.sqrt(D)
        attn = jnp.einsum('bhqd,bhkd->bhqk', q, k) / scale
        causal = jnp.tril(jnp.ones((Tx, Tx), dtype=bool))
        attn = jnp.where(causal[None, None], attn, -jnp.inf)
        attn = jax.nn.softmax(attn, axis=-1)
        out = jnp.einsum('bhqk,bhkd->bhqd', attn, v)
        out = out.transpose(0, 2, 1, 3).reshape(Bx, Tx, C)
        return out @ Wo.T

    def _L1_ffn_ref(x, w_gate, w_up, w_down):
        import jax, jax.numpy as jnp
        import numpy as np
        DIM_IN = 256
        DIM_HIDDEN = 1024
        gate = jnp.einsum('bsd,hd->bsh', x, w_gate)
        up = jnp.einsum('bsd,hd->bsh', x, w_up)
        gated = jax.nn.silu(gate) * up
        return jnp.einsum('bsh,dh->bsd', gated, w_down)
    x = L0_attn_x
    xn = _layernorm(x, axis=-1)
    x = x + _L0_attn_ref(xn, L0_attn_Wq, L0_attn_Wk, L0_attn_Wv, L0_attn_Wo) + _L0_ffn_ref(xn, L0_ffn_gate_w, L0_ffn_w_gate, L0_ffn_w_up, L0_ffn_w_down)
    xn = _layernorm(x, axis=-1)
    x = x + _L1_attn_ref(xn, L1_attn_Wq, L1_attn_Wk, L1_attn_Wv, L1_attn_Wo) + _L1_ffn_ref(xn, L1_ffn_w_gate, L1_ffn_w_up, L1_ffn_w_down)
    return x

_drawn_inputs = setup_inputs


def setup_inputs(seed=0):
    import zlib

    import numpy as np

    out = dict(_drawn_inputs(seed))
    spreads = {}
    factors = {'L0_attn_Wq': 8.0,
     'L0_attn_Wk': 8.0,
     'L0_attn_Wv': 6.77,
     'L0_attn_Wo': 6.754,
     'L0_ffn_gate_w': 8.0,
     'L0_ffn_w_gate': 8.0,
     'L0_ffn_w_up': 8.0,
     'L0_ffn_w_down': 8.0}
    for name, (base, spread) in spreads.items():
        noise = np.random.default_rng([zlib.crc32(name.encode()), seed]).standard_normal(out[name].shape)
        drawn = base * np.exp(spread * noise) if base else spread * noise
        out[name] = jnp.asarray(drawn.astype(out[name].dtype))
    for name, factor in factors.items():
        out[name] = (out[name] * factor).astype(out[name].dtype)
    return out
```

```python
from contextlib import ExitStack

import concourse.bass as bass
from concourse import mybir

F32 = mybir.dt.float32
BF16 = mybir.dt.bfloat16
I32 = mybir.dt.int32
U32 = mybir.dt.uint32
ALU = mybir.AluOpType
ACT = mybir.ActivationFunctionType
AX = mybir.AxisListType

P = 128
B, T, D = 4, 256, 256
H, DH = 16, 16
JT = T // P
NT = B * JT
DC = D // P
E, TOPK, F = 64, 8, 96
CAP = 2 * (B * T * TOPK) // E
SC = CAP // P
HID = 1024
HC = HID // P
LAYERS = 2
STEPS = B + 2
SCALE = (1.0 / T ** 0.5, 1.0 / DH ** 0.5)
EPS = 1e-5
NEG = -1e30
LOW = -3e38
V1 = DH + 1
PARTS_K = (0, 1, 2, 0, 1, 0)
PARTS_Q = (0, 0, 0, 1, 1, 2)
KS = len(PARTS_K) * DH
KM = KS + 3
NOWHERE = 1 << 16
RING = 4
BASE = 4
UNITS = 12


class Turns:

    def __init__(self):
        self.n = 0

    def next(self):
        self.n += 1
        return self.n - 1


def build(nc, x_in, wq0, wk0, wv0, wo0, gate_w, e_gate, e_up, e_down, wq1, wk1, wv1, wo1, f_gate, f_up, f_down, out):
    with ExitStack() as ctx:
        def sb(name, shape, dt=F32):
            return ctx.enter_context(nc.sbuf_tensor(name, shape, dt))

        def sem(name):
            return ctx.enter_context(nc.semaphore(name))

        def dram(name, shape, dt):
            return nc.dram_tensor(name, shape, dt, kind="Internal").ap()

        qk_dram = dram("qk_parts", [LAYERS * B, 2, 3, D, T], BF16)
        xn_dram = dram("xn_rows", [B * T, D], F32)
        table_dram = dram("slot_table", [E * CAP, 1], I32)
        y_dram = dram("expert_rows", [E * CAP, D], F32)

        x = sb("x", [P, NT, D])
        xn = sb("xn", [P, NT, D])
        xnT = sb("xnT", [P, DC, B * T])
        w_attn = [sb(f"w_attn{n}", [P, DC, D]) for n in range(8)]
        gwT = sb("gwT", [P, DC, E])
        wg1 = sb("wg1", [P, DC, HID])
        wu1 = sb("wu1", [P, DC, HID])
        wd1 = sb("wd1", [P, HC, D])
        identf = sb("identf", [P, P])
        later_f = sb("later_f", [P, P])
        ones_f = sb("ones_f", [P, P])
        identb = sb("identb", [P, P], BF16)
        mask_q = sb("mask_q", [P, P], BF16)
        mask_k = sb("mask_k", [P, P], BF16)
        earlier_b = sb("earlier_b", [P, P], BF16)
        ones_b = sb("ones_b", [P, P], BF16)
        floor = sb("floor", [P, LAYERS * JT])
        eps = sb("eps", [P, 1])
        e_idx = sb("e_idx", [P, E])
        e_base = sb("e_base", [P, E])
        tok_id = sb("tok_id", [P, NT], I32)
        nowhere = sb("nowhere", [P, P], I32)
        stats = sb("stats", [P, NT, 6])
        mv = sb("mv", [P, NT, 2])
        std = sb("std", [P, NT])
        rstd = sb("rstd", [P, NT])
        parts = [sb(f"parts{n}", [P, 3, DC, T], BF16) for n in range(2)]
        rest = [sb(f"rest{n}", [P, DC, T]) for n in range(2)]
        qs = [sb(f"qs{n}", [P, H, T], BF16) for n in range(2)]
        ks = [sb(f"ks{n}", [P, H, T], BF16) for n in range(2)]
        v1 = sb("v1", [P, NT * H, V1])
        mx = sb("mx", [P, JT, H])
        nm = sb("nm", [P, JT, P])
        nmc = sb("nmc", [P, JT, H])
        expn = sb("expn", [P, JT, H])
        nms = sb("nms", [H, 3, T], BF16)
        nmr = sb("nmr", [H, T])
        nmr2 = sb("nmr2", [H, T])
        p0 = sb("p0", [P, H, T])
        p1 = sb("p1", [P, H, P])
        num = sb("num", [P, H, V1])
        rec = sb("rec", [P, H])
        attn = sb("attn", [P, JT, D])
        attnT = sb("attnT", [P, DC, T])
        rmax = sb("rmax", [P, NT])
        rsum = sb("rsum", [P, NT])
        rrec = sb("rrec", [P, NT])
        prob = sb("prob", [P, NT, E])
        rep = sb("rep", [P, NT, E])
        dest = sb("dest", [P, NT, E])
        top = sb("top", [P, NT, TOPK])
        topi = sb("topi", [P, NT, TOPK], U32)
        topf = sb("topf", [P, NT, TOPK])
        chosen = sb("chosen", [P, NT, E], BF16)
        destk = sb("destk", [P, NT, TOPK])
        desti = sb("desti", [P, NT, TOPK], I32)
        wts = sb("wts", [P, NT, TOPK])
        tab_i = sb("tab_i", [P, P], I32)
        tab_f = sb("tab_f", [P, P])
        slots = sb("slots", [P, P], I32)
        wgu = [sb(f"wgu{n}", [P, 2, DC, F]) for n in range(RING)]
        wdn = [sb(f"wdn{n}", [F, D]) for n in range(RING)]
        xg = [sb(f"xg{n}", [P, SC, D]) for n in range(RING)]
        xT = [sb(f"xT{n}", [P, DC, CAP]) for n in range(2)]
        sg = [sb(f"sg{n}", [P, CAP]) for n in range(2)]
        hh = [sb(f"hh{n}", [P, CAP]) for n in range(2)]
        ysb = [sb(f"ysb{n}", [P, SC, D]) for n in range(RING)]
        yg = [p0[:, n * 8:(n + 1) * 8, :] for n in range(2)]

        bank = ctx.enter_context(nc.psum_tensor("bank", [P, 8, 512], F32))
        MX, ST, PD, PA, AC = (0, 1), (2, 3), (4, 5), 6, 7

        def bk(n, lo=0, hi=512):
            return bank[:, n, lo:hi]

        s_x = [sem(f"x_in{b}") for b in range(B)]
        s_w = [sem(f"w_in{n}") for n in range(12)]
        s_const = sem("const_ready")
        s_now = sem("nowhere_ready")
        s_set = sem("tiles_set")
        s_yz = sem("rows_back_zeroed")
        s_c0 = sem("const_zeroed")
        s_tab0 = sem("table_filled")
        s_stat = sem("stats_done")
        s_mv = sem("moments_done")
        s_std = sem("std_done")
        s_rstd = sem("rstd_done")
        s_xn = sem("xn_done")
        s_xnst = sem("xn_stored")
        s_pa = sem("pa_full")
        s_paf = sem("pa_drained")
        s_pd = sem("pd_full")
        s_pdf = sem("pd_drained")
        s_mxf = sem("max_bank_full")
        s_mxd = sem("max_bank_drained")
        s_st = sem("score_bank_full")
        s_exp = sem("exp_done")
        s_hi = sem("hi_done")
        s_mid = sem("mid_done")
        s_lo = sem("lo_done")
        s_qkst = sem("qk_stored")
        s_stack = [sem(f"stack_in{n}") for n in range(2)]
        s_nm = sem("neg_max_done")
        s_nmc = sem("neg_max_clamped")
        s_nms = sem("neg_max_parts_done")
        s_nmrow = sem("neg_max_rows_in")
        s_nch = sem("neg_max_chain")
        s_expn = sem("exp_neg_max_done")
        s_ach = sem("attend_chain")
        s_attn = sem("attn_done")
        s_oadd = sem("attn_added")
        s_lg = sem("logits_done")
        s_rch = sem("router_chain")
        s_rsh = sem("router_shifted")
        s_rexp = sem("router_exp_done")
        s_chosen = sem("chosen_done")
        s_pos = sem("positions_done")
        s_dest = sem("dest_done")
        s_scat = sem("scattered")
        s_tab = sem("table_read")
        s_tabf = sem("table_float")
        s_tabT = sem("table_turned")
        s_slots = sem("slots_done")
        s_wts = [sem(f"expert_w{n}") for n in range(RING)]
        s_xg = [sem(f"expert_x{n}") for n in range(RING)]
        s_yst = [sem(f"expert_y{n}") for n in range(RING)]
        s_xTp = sem("expert_xT_psum")
        s_xT = sem("expert_xT")
        s_gu = sem("expert_gu")
        s_sg = sem("expert_silu")
        s_h = sem("expert_h")
        s_yp = sem("expert_y_psum")
        s_y = sem("expert_y")
        s_yg = [sem(f"rows_back{n}") for n in range(2)]
        s_comb = sem("combine_chain")
        s_fsg = sem("ffn_silu")
        s_fh = sem("ffn_h")
        s_fdn = sem("ffn_down")
        s_fadd = sem("ffn_added")
        s_out = sem("out_stored")

        block = ctx.enter_context(nc.Block())

        def tiles(b):
            return slice(JT * b, JT * b + JT)

        def steps(L):
            for s in range(STEPS):
                yield s, (L * B + s), s >= 2, 1 <= s <= B, s < B

        def unit_heads(u):
            if u < 8:
                return range(2 * u, 2 * u + 2), T
            return range(4 * (u - 8), 4 * (u - 8) + 4), P

        CONSTS = 4 + 6 + 1 + 3
        SETS = 4 + RING

        @block.sync
        def _(sp):
            xv = x_in.rearrange("b (j p) d -> p b j d", p=P)
            for b in range(B):
                sp.dma_start(x[:, tiles(b), :], xv[:, b]).then_inc(s_x[b], 16)
            for n, w in enumerate((wq0, wk0, wv0, wo0)):
                sp.dma_start(w_attn[n][:], w.rearrange("(c p) n -> p c n", p=P)).then_inc(s_w[n], 16)
            sp.dma_start(gwT[:], gate_w.rearrange("(c p) n -> p c n", p=P)).then_inc(s_w[8], 16)
            sp.wait_ge(s_now, 1)
            sp.dma_start(table_dram.rearrange("(r c) one -> r (c one)", c=P), nowhere[:]).then_inc(s_tab0, 16)
            sp.wait_ge(s_xn, NT)
            sp.dma_start(xn_dram.rearrange("(t p) d -> p t d", p=P), xn[:]).then_inc(s_xnst, 16)

            def expert_weights(e, j):
                sp.dma_start(wgu[j][:, 0], e_gate[e]).then_inc(s_wts[j], 16)
                sp.dma_start(wgu[j][:, 1], e_up[e]).then_inc(s_wts[j], 16)
                sp.dma_start(wdn[j][:], e_down[e]).then_inc(s_wts[j], 16)

            def attention_moves(L):
                for s, g, attends, maxes, projects in steps(L):
                    if maxes:
                        m = g - 1
                        sp.wait_ge(s_nms, m + 1)
                        for r in range(3):
                            sp.dma_start(qs[m % 2][KS + r:KS + r + 1, :, :], nms[:, r, :]).then_inc(s_nmrow, 16)
                    if projects:
                        sp.wait_ge(s_lo, 2 * g + 2)
                        for n in range(2):
                            sp.dma_start(qk_dram[g, n].rearrange("s (m p) t -> p (s m) t", p=P),
                                         parts[n][:].rearrange("p s m t -> p (s m) t")).then_inc(s_qkst, 16)
                        sp.wait_ge(s_qkst, 32 * (g + 1))
                        if g >= 2:
                            sp.wait_ge(s_st, UNITS * (g - 1))
                        for stack, n, order in ((qs, 0, PARTS_Q), (ks, 1, PARTS_K)):
                            for r, part in enumerate(order):
                                sp.dma_start(stack[g % 2][r * DH:(r + 1) * DH, :, :],
                                             qk_dram[g, n, part].rearrange("(h d) t -> d h t", d=DH)
                                             ).then_inc(s_stack[g % 2], 16)

            attention_moves(0)
            for n, w in enumerate((wq1, wk1, wv1, wo1)):
                sp.dma_start(w_attn[4 + n][:], w.rearrange("(c p) n -> p c n", p=P)).then_inc(s_w[4 + n], 16)
            for n, (tile, w) in enumerate(((wg1, f_gate), (wu1, f_up), (wd1, f_down))):
                sp.dma_start(tile[:], w.rearrange("(c p) n -> p c n", p=P)).then_inc(s_w[9 + n], 16)
            for j in range(RING):
                expert_weights(j, j)
            sp.wait_ge(s_scat, 16 * NT * TOPK)
            sp.dma_start(tab_i[:], table_dram.rearrange("(r c) one -> r (c one)", c=P)).then_inc(s_tab, 16)

            def store_rows(e, j):
                sp.wait_ge(s_y, BASE + 1 + e)
                sp.dma_start(y_dram.rearrange("(e c p) d -> e p c d", e=E, p=P)[e], ysb[j][:]).then_inc(s_yst[j], 16)

            with sp.Fori(0, E // RING - 1) as i:
                for j in range(RING):
                    store_rows(i * RING + j, j)
                    expert_weights(i * RING + j + RING, j)
            for j in range(RING):
                store_rows(E - RING + j, j)
            attention_moves(1)
            for b in range(B):
                sp.wait_ge(s_oadd, B + b + 1)
                sp.dma_start(out.rearrange("b (j p) d -> p b j d", p=P)[:, b], x[:, tiles(b), :]).then_inc(s_out, 16)
            sp.wait_ge(s_out, 16 * B)

        @block.gpsimd
        def _(pool):
            pool.memset(nowhere[:], NOWHERE).then_inc(s_now, 1)
            for tile in (identf, later_f, identb, mask_q, mask_k, earlier_b):
                pool.memset(tile[:], 0.0).then_inc(s_c0, 1)
            pool.memset(floor[:, 0:JT], 0.0).then_inc(s_c0, 1)
            pool.memset(ones_f[:], 1.0).then_inc(s_const, 1)
            pool.memset(ones_b[:], 1.0).then_inc(s_const, 1)
            pool.memset(floor[:, JT:], LOW).then_inc(s_const, 1)
            pool.memset(eps[:], EPS).then_inc(s_const, 1)
            pool.wait_ge(s_c0, 7)
            diag = dict(compare_op=ALU.not_equal, pattern=[[-1, P]], base=0, channel_multiplier=1)
            row_ge = dict(compare_op=ALU.is_ge, pattern=[[-1, P]], base=0, channel_multiplier=1)
            col_ge = dict(compare_op=ALU.is_ge, pattern=[[1, P]], base=0, channel_multiplier=-1)
            for tile, where, fill in ((identf, diag, 1.0), (identb, diag, 1.0), (later_f, col_ge, 1.0),
                                      (mask_q, row_ge, NEG), (mask_k, col_ge, NEG), (earlier_b, row_ge, 1.0)):
                pool.affine_select(out=tile[:], in_=tile[:], fill=fill, **where).then_inc(s_const, 1)
            pool.affine_select(out=floor[:, JT - 1:JT], in_=floor[:, JT - 1:JT], compare_op=ALU.not_equal, fill=LOW,
                               pattern=[[0, 1]], base=-(P - 1), channel_multiplier=1).then_inc(s_const, 1)
            pool.iota(e_idx[:], [[1, E]], base=0, channel_multiplier=0, allow_small_or_imprecise_dtypes=True
                      ).then_inc(s_const, 1)
            pool.iota(e_base[:], [[CAP, E]], base=0, channel_multiplier=0, allow_small_or_imprecise_dtypes=True
                      ).then_inc(s_const, 1)
            pool.iota(tok_id[:], [[P, NT]], base=0, channel_multiplier=1).then_inc(s_const, 1)

            pool.wait_ge(s_set, SETS)
            pool.wait_ge(s_dest, 1)
            pool.wait_ge(s_tab0, 16)
            for t in range(NT):
                for k in range(TOPK):
                    pool.indirect_dma_start(table_dram, bass.IndirectOffsetOnAxis(desti[:, t, k:k + 1], 0),
                                            tok_id[:, t:t + 1], None, bounds_check=E * CAP - 1, oob_is_err=False
                                            ).then_inc(s_scat, 16)
            pool.wait_ge(s_slots, 1)
            pool.wait_ge(s_xnst, 16)
            for e in range(E):
                if e >= RING:
                    pool.wait_ge(s_xTp, BASE + 1 + e - RING)
                for c in range(SC):
                    pool.indirect_dma_start(xg[e % RING][:, c, :], None, xn_dram,
                                            bass.IndirectOffsetOnAxis(slots[:, e * SC + c:e * SC + c + 1], 0),
                                            bounds_check=B * T - 1, oob_is_err=False).then_inc(s_xg[e % RING], 16)
            for n in range(2):
                pool.memset(yg[n], 0.0).then_inc(s_yz, 1)
            pool.wait_ge(s_yz, 2)
            for j in range(RING):
                pool.wait_ge(s_yst[j], 16 * (E // RING))
            for t in range(NT):
                if t >= 2:
                    pool.wait_ge(s_comb, TOPK * (t - 1))
                for k in range(TOPK):
                    pool.indirect_dma_start(yg[t % 2][:, k, :], None, y_dram,
                                            bass.IndirectOffsetOnAxis(desti[:, t, k:k + 1], 0),
                                            bounds_check=E * CAP - 1, oob_is_err=False).then_inc(s_yg[t % 2], 16)

        @block.tensor
        def _(pe):
            pd, pa, mt, stt = Turns(), Turns(), Turns(), Turns()

            def take_pd():
                n = pd.next()
                if n >= 2:
                    pe.wait_ge(s_pdf, n - 1)
                return PD[n % 2]

            def take_pa():
                n = pa.next()
                if n >= 1:
                    pe.wait_ge(s_paf, n)
                return PA

            def turn(b):
                pe.wait_ge(s_xn, NT * (g_layer[0]) + JT * (b + 1))
                bn = take_pa()
                for c in range(DC):
                    for j in range(JT):
                        last = pe.transpose(bk(bn, c * T + j * P, c * T + (j + 1) * P),
                                            xn[:, JT * b + j, c * P:(c + 1) * P], identf[:])
                last.then_inc(s_pa, 1)

            g_layer = [0]

            def project(L, b, g):
                for n in range(2):
                    bn = take_pd()
                    if b == 0:
                        pe.wait_ge(s_w[4 * L + n], 16)
                    for m in range(DC):
                        for c in range(DC):
                            last = pe.matmul(bk(bn, m * T, (m + 1) * T), w_attn[4 * L + n][:, c, m * P:(m + 1) * P],
                                             xnT[:, c, b * T:(b + 1) * T], start=c == 0, stop=c == DC - 1)
                    last.then_inc(s_pd, 1)
                bn = take_pa()
                if b == 0:
                    pe.wait_ge(s_w[4 * L + 2], 16)
                for j in range(JT):
                    for c in range(DC):
                        last = pe.matmul(bk(bn, j * D, (j + 1) * D),
                                         xnT[:, c, b * T + j * P:b * T + (j + 1) * P], w_attn[4 * L + 2][:, c, :],
                                         start=c == 0, stop=c == DC - 1)
                last.then_inc(s_pa, 1)

            def maxima(g):
                pe.wait_ge(s_stack[g % 2], 16 * 12 * (g // 2 + 1))
                for u in range(UNITS):
                    n = mt.next()
                    if n >= 2:
                        pe.wait_ge(s_mxd, n - 1)
                    heads, w = unit_heads(u)
                    q0 = T - w if w == P else T - P
                    if w == P:
                        q0 = 0
                    for i, h in enumerate(heads):
                        o = i * w
                        pe.matmul(bk(MX[n % 2], o, o + w), qs[g % 2][0:KS, h, q0:q0 + P], ks[g % 2][0:KS, h, 0:w],
                                  start=True, stop=False)
                        last = pe.matmul(bk(MX[n % 2], o + w - P, o + w), identb[:], mask_q[:],
                                         start=False, stop=True)
                    last.then_inc(s_mxf, 1)

            def attend(L, b, g):
                pe.wait_ge(s_nmrow, 48 * (g + 1))
                for u in range(UNITS):
                    n = stt.next()
                    if n >= 2:
                        pe.wait_ge(s_exp, n - 1)
                    heads, w = unit_heads(u)
                    k0 = 0 if w == T else P
                    for i, h in enumerate(heads):
                        o = i * w
                        pe.matmul(bk(ST[n % 2], o, o + w), ks[g % 2][0:KM, h, k0:k0 + P], qs[g % 2][0:KM, h, T - w:T],
                                  start=True, stop=False)
                        last = pe.matmul(bk(ST[n % 2], o, o + P), identb[:], mask_k[:], start=False, stop=True)
                    last.then_inc(s_st, 1)
                for j in range(JT):
                    if L == 0:
                        bn = take_pd()
                        pe.matmul(bk(bn, 0, H * V1), later_f[:], v1[:, (JT * b + j) * H:(JT * b + j + 1) * H, :],
                                  start=True, stop=j == JT - 1)
                        last = None
                        if j == 0:
                            pe.matmul(bk(bn, 0, H * V1), ones_f[:], v1[:, (JT * b + 1) * H:(JT * b + 2) * H, :],
                                      start=False, stop=True).then_inc(s_pd, 1)
                        else:
                            pe.matmul(bk(bn, H * V1, H * V1 + 1), ones_f[:], ones_f[:, 0:1],
                                      start=True, stop=True).then_inc(s_pd, 1)
                    bn = take_pd()
                    for h in range(H):
                        if j == 0:
                            pe.wait_ge(s_exp, UNITS * g + h // 2 + 1)
                        else:
                            pe.wait_ge(s_exp, UNITS * g + 8 + h // 4 + 1)
                        o = bk(bn, h * V1, (h + 1) * V1)
                        last = pe.matmul(o, p0[:, h, j * P:(j + 1) * P], v1[:, JT * b * H + h, :],
                                         start=True, stop=j == 0)
                        if j == 1:
                            last = pe.matmul(o, p1[:, h, :], v1[:, (JT * b + 1) * H + h, :], start=False, stop=True)
                    last.then_inc(s_pd, 1)

            def output(L, b, g):
                pe.wait_ge(s_attn, JT * (g + 1))
                bn = take_pa()
                for c in range(DC):
                    for j in range(JT):
                        last = pe.transpose(bk(bn, c * T + j * P, c * T + (j + 1) * P),
                                            attn[:, j, c * P:(c + 1) * P], identf[:])
                last.then_inc(s_pa, 1)
                pe.wait_ge(s_paf, pa.n)
                bn = take_pd()
                if b == 0:
                    pe.wait_ge(s_w[4 * L + 3], 16)
                for j in range(JT):
                    for c in range(DC):
                        last = pe.matmul(bk(bn, j * D, (j + 1) * D), attnT[:, c, j * P:(j + 1) * P],
                                         w_attn[4 * L + 3][:, c, :], start=c == 0, stop=c == DC - 1)
                last.then_inc(s_pd, 1)

            def turn_maxima(g):
                pe.wait_ge(s_nm, g + 1)
                bn = take_pd()
                for j in range(JT):
                    last = pe.transpose(bk(bn, j * P, (j + 1) * P), nm[:, j, :], identf[:])
                last.then_inc(s_pd, 1)

            def ffn(b):
                def down(hc):
                    m = HC * b + hc
                    pe.wait_ge(s_fh, m + 1)
                    if hc == 0 and b > 0:
                        pe.wait_ge(s_fadd, b)
                    for j in range(JT):
                        last = pe.matmul(bk(AC, j * D, (j + 1) * D), hh[m % 2][:, j * P:(j + 1) * P], wd1[:, hc, :],
                                         start=hc == 0 and j == 0, stop=hc == HC - 1, skip_group_check=True)
                    last.then_inc(s_fdn, 1)

                for n in range(3):
                    pe.wait_ge(s_w[9 + n], 16)
                for hc in range(HC):
                    bn = take_pd()
                    for n, w in enumerate((wg1, wu1)):
                        for c in range(DC):
                            last = pe.matmul(bk(bn, n * T, (n + 1) * T), w[:, c, hc * P:(hc + 1) * P],
                                             xnT[:, c, b * T:(b + 1) * T], start=c == 0, stop=c == DC - 1)
                    last.then_inc(s_pd, 1)
                    if hc >= 1:
                        down(hc - 1)
                down(HC - 1)

            pe.wait_ge(s_const, CONSTS)
            pe.wait_ge(s_set, SETS)
            for b in range(B):
                turn(b)
            pe.wait_ge(s_w[8], 16)
            for b in range(B):
                pe.wait_ge(s_paf, b + 1)
                for t in range(JT * b, JT * b + JT):
                    for c in range(DC):
                        last = pe.matmul(bk(AC, t * E, (t + 1) * E), xnT[:, c, t * P:(t + 1) * P], gwT[:, c, :],
                                         start=c == 0, stop=c == DC - 1)
            last.then_inc(s_lg, 1)

            def positions():
                pe.wait_ge(s_chosen, 1)
                for t in range(NT):
                    o = bk(AC, t * E, (t + 1) * E)
                    for before in range(t):
                        pe.matmul(o, ones_b[:], chosen[:, before, :], start=before == 0, stop=False)
                    last = pe.matmul(o, earlier_b[:], chosen[:, t, :], start=t == 0, stop=True)
                last.then_inc(s_pos, 1)

            for s, g, attends, maxes, projects in steps(0):
                if attends:
                    attend(0, s - 2, g - 2)
                if maxes:
                    maxima(g - 1)
                if attends:
                    output(0, s - 2, g - 2)
                if maxes:
                    turn_maxima(g - 1)
                if projects:
                    project(0, s, g)
                if s == 0:
                    positions()

            pe.wait_ge(s_tabf, 1)
            pe.transpose(bk(AC, 0, P), tab_f[:], identf[:]).then_inc(s_tabT, 1)
            pe.wait_ge(s_mxd, mt.n)
            pe.wait_ge(s_exp, stt.n)
            pe.wait_ge(s_pdf, pd.n)

            def e_turn(e, j, i):
                pe.wait_ge(s_xg[j], 16 * SC * (i + 1))
                pe.wait_ge(s_xT, e + BASE + 1 - 2)
                for c in range(DC):
                    for k in range(SC):
                        last = pe.transpose(bk(MX[j % 2], c * CAP + k * P, c * CAP + (k + 1) * P),
                                            xg[j][:, k, c * P:(c + 1) * P], identf[:])
                last.then_inc(s_xTp, 1)

            def e_gate_up(e, j, i):
                pe.wait_ge(s_xT, e + BASE + 1)
                pe.wait_ge(s_wts[j], 48 * (i + 1))
                pe.wait_ge(s_h, e + BASE + 1 - 2)
                for n in range(2):
                    for c in range(DC):
                        last = pe.matmul(bank[0:F, ST[j % 2], n * CAP:(n + 1) * CAP], wgu[j][:, n, c, :],
                                         xT[j % 2][:, c, :], start=c == 0, stop=c == DC - 1)
                last.then_inc(s_gu, 1)

            def e_down_(e, j, i):
                pe.wait_ge(s_h, e + BASE + 1)
                pe.wait_ge(s_y, e + BASE + 1 - 2)
                for k in range(SC):
                    last = pe.matmul(bk(PD[j % 2], k * D, (k + 1) * D), hh[j % 2][0:F, k * P:(k + 1) * P], wdn[j][:],
                                     start=True, stop=True)
                last.then_inc(s_yp, 1)

            pe.sem_inc(s_xTp, BASE)
            pe.sem_inc(s_gu, BASE)
            pe.sem_inc(s_yp, BASE)
            e_turn(0, 0, 0)
            e_turn(1, 1, 0)
            e_gate_up(0, 0, 0)
            with pe.Fori(0, E // RING - 1) as i:
                for j in range(RING):
                    e = i * RING + j
                    e_turn(e + 2, (j + 2) % RING, i + (j + 2) // RING)
                    e_gate_up(e + 1, (j + 1) % RING, i + (j + 1) // RING)
                    e_down_(e, j, i)
            for e in range(E - RING, E):
                if e + 2 < E:
                    e_turn(e + 2, (e + 2) % RING, (e + 2) // RING)
                if e + 1 < E:
                    e_gate_up(e + 1, (e + 1) % RING, (e + 1) // RING)
                e_down_(e, e % RING, e // RING)
            pe.wait_ge(s_y, E + BASE)

            g_layer[0] = 1
            for s, g, attends, maxes, projects in steps(1):
                if attends:
                    attend(1, s - 2, g - 2)
                if maxes:
                    maxima(g - 1)
                if attends:
                    output(1, s - 2, g - 2)
                if maxes:
                    turn_maxima(g - 1)
                if projects:
                    turn(s)
                    pe.wait_ge(s_paf, pa.n)
                    project(1, s, g)
                    ffn(s)

        @block.scalar
        def _(act):
            pd, pa, stt = Turns(), Turns(), Turns()

            def drain_pa(dst, src_shape):
                n = pa.next()
                act.wait_ge(s_pa, n + 1)
                act.activation(dst, bk(PA).rearrange("p (a b) -> p a b", a=src_shape), ACT.Copy).then_inc(s_paf, 1)

            def std_of(L, b):
                act.wait_ge(s_mv, NT * L + JT * (b + 1))
                act.activation(std[:, tiles(b)], mv[:, tiles(b), 1], ACT.Sqrt, bias=eps[:]).then_inc(s_std, 1)

            def attend(L, b, g):
                for u in range(UNITS):
                    n = stt.next()
                    act.wait_ge(s_st, n + 1)
                    if u == 0 and g > 0:
                        act.wait_ge(s_attn, JT * g)
                    heads, w = unit_heads(u)
                    dst = (p0 if w == T else p1)[:, heads[0]:heads[-1] + 1, :]
                    act.activation(dst, bk(ST[n % 2]).rearrange("p (a b) -> p a b", b=w), ACT.Exp,
                                   scale=SCALE[L]).then_inc(s_exp, 1)
                pd.n += 4 if L == 0 else 2

            def exp_neg_max(L, g):
                if L == 0:
                    act.wait_ge(s_nmc, g + 1)
                    act.activation(expn[:], nmc[:], ACT.Exp, scale=SCALE[L]).then_inc(s_expn, 1)

            def project(b, g):
                full = []
                for n in range(2):
                    full.append(pd.next())
                    act.wait_ge(s_pd, full[n] + 1)
                    if g > 0:
                        act.wait_ge(s_qkst, 32 * g)
                    act.activation(parts[n][:, 0], bk(PD[full[n] % 2]).rearrange("p (m t) -> p m t", m=DC),
                                   ACT.Copy).then_inc(s_hi, 1)
                n = pa.next()
                act.wait_ge(s_pa, n + 1)
                act.activation(v1[:, JT * b * H:JT * (b + 1) * H, 0:DH],
                               bk(PA).rearrange("p (a d) -> p a d", d=DH), ACT.Copy).then_inc(s_paf, 1)
                for n in range(2):
                    act.wait_ge(s_pdf, full[n] + 1)
                    act.activation(parts[n][:, 1], rest[n][:], ACT.Copy).then_inc(s_mid, 1)

            def ffn(b):
                for hc in range(HC):
                    m = HC * b + hc
                    n = pd.next()
                    act.wait_ge(s_pd, n + 1)
                    if m >= 2:
                        act.wait_ge(s_fh, m - 1)
                    act.activation(sg[m % 2][:], bk(PD[n % 2], 0, T), ACT.Silu).then_inc(s_fsg, 1)

            act.wait_ge(s_const, CONSTS)
            act.wait_ge(s_set, SETS)
            for b in range(B):
                std_of(0, b)
            for b in range(B):
                drain_pa(xnT[:, :, b * T:(b + 1) * T], DC)
            act.wait_ge(s_rsh, 1)
            act.activation(prob[:], rep[:], ACT.Exp).then_inc(s_rexp, 1)
            for s, g, attends, maxes, projects in steps(0):
                if attends:
                    attend(0, s - 2, g - 2)
                    act.wait_ge(s_oadd, g - 2)
                    drain_pa(attnT[:], DC)
                    pd.n += 1
                if maxes:
                    exp_neg_max(0, g - 1)
                    pd.n += 1
                if projects:
                    project(s, g)

            def silu(e, j):
                act.wait_ge(s_gu, e + BASE + 1)
                act.wait_ge(s_h, e + BASE + 1 - 2)
                act.activation(sg[j % 2][0:F, :], bank[0:F, ST[j % 2], 0:CAP], ACT.Silu).then_inc(s_sg, 1)

            def rows_out(e, j, i):
                act.wait_ge(s_yp, e + BASE + 1)
                act.wait_ge(s_yst[j], 16 * i)
                act.activation(ysb[j][:], bk(PD[j % 2]).rearrange("p (c d) -> p c d", c=SC), ACT.Copy
                               ).then_inc(s_y, 1)

            act.sem_inc(s_sg, BASE)
            act.sem_inc(s_y, BASE)
            silu(0, 0)
            with act.Fori(0, E // RING - 1) as i:
                for j in range(RING):
                    silu(i * RING + j + 1, (j + 1) % RING)
                    rows_out(i * RING + j, j, i)
            for e in range(E - RING, E):
                if e + 1 < E:
                    silu(e + 1, (e + 1) % RING)
                rows_out(e, e % RING, e // RING)

            for s, g, attends, maxes, projects in steps(1):
                if attends:
                    attend(1, s - 2, g - 2)
                    act.wait_ge(s_oadd, g - 2)
                    drain_pa(attnT[:], DC)
                    pd.n += 1
                if maxes:
                    pd.n += 1
                if projects:
                    std_of(1, s)
                    drain_pa(xnT[:, :, s * T:(s + 1) * T], DC)
                    project(s, g)
                    ffn(s)

        @block.vector
        def _(dve):
            pd, mt = Turns(), Turns()
            nch, ach, rch, lch = Turns(), Turns(), Turns(), Turns()

            def link(ins, s, turns):
                turns.next()
                ins.then_inc(s, 1)
                dve.wait_ge(s, turns.n)

            def moments(L, b):
                for t in range(JT * b, JT * b + JT):
                    dve.bn_stats(stats[:, t, :], x[:, t, :]).then_inc(s_stat, 1)
                dve.wait_ge(s_stat, NT * L + JT * (b + 1))
                for t in range(JT * b, JT * b + JT):
                    dve.bn_aggr(mv[:, t, :], stats[:, t, :]).then_inc(s_mv, 1)

            def normalise(L, b):
                dve.wait_ge(s_std, B * L + b + 1)
                dve.wait_ge(s_mv, NT * L + JT * (b + 1))
                dve.reciprocal(rstd[:, tiles(b)], std[:, tiles(b)]).then_inc(s_rstd, 1)
                dve.wait_ge(s_rstd, B * L + b + 1)
                for t in range(JT * b, JT * b + JT):
                    dve.tensor_scalar(xn[:, t, :], x[:, t, :], mv[:, t, 0:1], rstd[:, t:t + 1],
                                      ALU.subtract, ALU.mult).then_inc(s_xn, 1)

            def maxima(L, g):
                if g > 0:
                    dve.wait_ge(s_nm, g)
                for u in range(UNITS):
                    n = mt.next()
                    heads, w = unit_heads(u)
                    dve.wait_ge(s_mxf, n + 1)
                    dve.reduce_max(mx[:, 1 if w == T else 0, heads[0]:heads[-1] + 1],
                                   bk(MX[n % 2]).rearrange("p (a b) -> p a b", b=w), AX.X).then_inc(s_mxd, 1)

            def negate(L, g):
                dve.wait_ge(s_mxd, UNITS * (g + 1))
                if L == 0 and g > 0:
                    dve.wait_ge(s_expn, g)
                for j in range(JT):
                    ins = dve.tensor_scalar(nm[:, j, 0:H], mx[:, j, :], floor[:, JT * L + j:JT * L + j + 1], -1.0,
                                            ALU.max, ALU.mult)
                ins.then_inc(s_nm, 1)
                if L == 0:
                    dve.wait_ge(s_nm, g + 1)
                    dve.tensor_scalar(nmc[:], nm[:, :, 0:H], 0.0, None, ALU.min).then_inc(s_nmc, 1)

            def split_maxima(g):
                n = pd.next()
                dve.wait_ge(s_pd, n + 1)
                if g > 0:
                    dve.wait_ge(s_nms, g)
                    dve.wait_ge(s_nmrow, 48 * g)
                src = bank[0:H, PD[n % 2], 0:T]
                link(dve.tensor_copy(nms[:, 0, :], src), s_nch, nch)
                dve.tensor_tensor(nmr[:], src, nms[:, 0, :], ALU.subtract).then_inc(s_pdf, 1)
                dve.wait_ge(s_pdf, n + 1)
                link(dve.tensor_copy(nms[:, 1, :], nmr[:]), s_nch, nch)
                dve.tensor_tensor(nms[:, 2, :], nmr[:], nms[:, 1, :], ALU.subtract).then_inc(s_nms, 1)

            def attend(L, b, g):
                for j in range(JT):
                    if JT * g + j > 0:
                        dve.wait_ge(s_attn, JT * g + j)
                    if L == 0:
                        dve.wait_ge(s_expn, g + 1)
                        n = pd.next()
                        dve.wait_ge(s_pd, n + 1)
                        dve.tensor_tensor(num[:], bk(PD[n % 2], 0, H * V1).rearrange("p (h d) -> p h d", d=V1),
                                          expn[:, j, :].unsqueeze(2).broadcast_to([P, H, V1]), ALU.mult
                                          ).then_inc(s_pdf, 1)
                        dve.wait_ge(s_pdf, n + 1)
                        n = pd.next()
                        dve.wait_ge(s_pd, n + 1)
                        dve.tensor_tensor(num[:], bk(PD[n % 2], 0, H * V1).rearrange("p (h d) -> p h d", d=V1),
                                          num[:], ALU.add).then_inc(s_pdf, 1)
                        dve.wait_ge(s_pdf, n + 1)
                        src = num[:]
                    else:
                        n = pd.next()
                        dve.wait_ge(s_pd, n + 1)
                        src = bk(PD[n % 2], 0, H * V1).rearrange("p (h d) -> p h d", d=V1)
                    link(dve.reciprocal(rec[:], src[:, :, DH]), s_ach, ach)
                    if g > 0:
                        dve.wait_ge(s_paf, att_pa(g - 1))
                    ins = dve.tensor_tensor(attn[:, j, :].rearrange("p (h d) -> p h d", d=DH), src[:, :, 0:DH],
                                            rec[:].unsqueeze(2).broadcast_to([P, H, DH]), ALU.mult)
                    ins.then_inc(s_attn, 1)
                    if L == 1:
                        dve.wait_ge(s_attn, JT * g + j + 1)
                        dve.engine_nop().then_inc(s_pdf, 1)

            def att_pa(g):
                return PA_USES[g]

            def output(b, g):
                n = pd.next()
                dve.wait_ge(s_pd, n + 1)
                dve.tensor_tensor(x[:, tiles(b), :], bk(PD[n % 2]).rearrange("p (j d) -> p j d", j=JT),
                                  x[:, tiles(b), :], ALU.add).then_inc(s_pdf, 1)
                dve.wait_ge(s_pdf, n + 1)
                dve.engine_nop().then_inc(s_oadd, 1)

            def project(g):
                full = [pd.next(), pd.next()]
                if g > 0:
                    dve.wait_ge(s_lo, 2 * g)
                for n in range(2):
                    dve.wait_ge(s_hi, 2 * g + n + 1)
                    dve.tensor_tensor(rest[n][:], bk(PD[full[n] % 2]).rearrange("p (m t) -> p m t", m=DC),
                                      parts[n][:, 0], ALU.subtract).then_inc(s_pdf, 1)
                for n in range(2):
                    dve.wait_ge(s_pdf, full[n] + 1)
                    dve.wait_ge(s_mid, 2 * g + n + 1)
                    dve.tensor_tensor(parts[n][:, 2], rest[n][:], parts[n][:, 1], ALU.subtract).then_inc(s_lo, 1)

            def router():
                lg = bk(AC).rearrange("p (t e) -> p t e", e=E)
                dve.wait_ge(s_lg, 1)
                link(dve.reduce_max(rmax[:], lg, AX.X), s_rch, rch)
                dve.tensor_tensor(rep[:], lg, rmax[:].unsqueeze(2).broadcast_to([P, NT, E]), ALU.subtract
                                  ).then_inc(s_rsh, 1)
                dve.wait_ge(s_rexp, 1)
                link(dve.reduce_sum(rsum[:], prob[:], AX.X), s_rch, rch)
                link(dve.reciprocal(rrec[:], rsum[:]), s_rch, rch)
                link(dve.tensor_tensor(prob[:], prob[:], rrec[:].unsqueeze(2).broadcast_to([P, NT, E]), ALU.mult),
                     s_rch, rch)
                for t in range(NT):
                    ins = dve.max(top[:, t, :], prob[:, t, :])
                link(ins, s_rch, rch)
                for t in range(NT):
                    dve.max_index(topi[:, t, :], top[:, t, :], prob[:, t, :])
                    ins = dve.match_replace(rep[:, t, :], top[:, t, :], prob[:, t, :], -1.0)
                link(ins, s_rch, rch)
                dve.tensor_scalar(chosen[:], rep[:], 0.0, None, ALU.is_lt).then_inc(s_chosen, 1)
                link(dve.tensor_copy(topf[:], topi[:]), s_rch, rch)

            def destinations():
                pos = bk(AC).rearrange("p (t e) -> p t e", e=E)
                dve.wait_ge(s_pos, 1)
                link(dve.tensor_scalar(dest[:], pos, float(CAP), float(NOWHERE), ALU.is_ge, ALU.mult), s_rch, rch)
                link(dve.tensor_tensor(dest[:], pos, dest[:], ALU.add), s_rch, rch)
                link(dve.tensor_tensor(dest[:], dest[:], e_base[:].unsqueeze(1).broadcast_to([P, NT, E]), ALU.add),
                     s_rch, rch)
                for k in range(TOPK):
                    link(dve.tensor_tensor(rep[:], e_idx[:].unsqueeze(1).broadcast_to([P, NT, E]),
                                           topf[:, :, k:k + 1].broadcast_to([P, NT, E]), ALU.is_equal), s_rch, rch)
                    link(dve.tensor_tensor(rep[:], rep[:], dest[:], ALU.mult), s_rch, rch)
                    link(dve.reduce_sum(destk[:, :, k], rep[:], AX.X), s_rch, rch)
                dve.tensor_copy(desti[:], destk[:]).then_inc(s_dest, 1)
                link(dve.scalar_tensor_tensor(wts[:], destk[:], float(NOWHERE), top[:], ALU.is_lt, ALU.mult),
                     s_rch, rch)

            for n in range(2):
                dve.memset(ks[n][KS:KM, :, :], 1.0).then_inc(s_set, 1)
            dve.memset(nm[:], 0.0).then_inc(s_set, 1)
            dve.memset(v1[:, :, DH:V1], 1.0).then_inc(s_set, 1)
            for n in range(RING):
                dve.memset(xg[n][:], 0.0).then_inc(s_set, 1)
            dve.wait_ge(s_const, CONSTS)
            dve.wait_ge(s_set, SETS)
            for b in range(B):
                dve.wait_ge(s_x[b], 16)
                moments(0, b)
            for b in range(B):
                normalise(0, b)
            router()
            for s, g, attends, maxes, projects in steps(0):
                if attends:
                    attend(0, s - 2, g - 2)
                if maxes:
                    maxima(0, g - 1)
                if attends:
                    output(s - 2, g - 2)
                if maxes:
                    negate(0, g - 1)
                    split_maxima(g - 1)
                if projects:
                    project(g)
                if s == 0:
                    destinations()

            dve.wait_ge(s_tab, 16)
            dve.tensor_copy(tab_f[:], tab_i[:]).then_inc(s_tabf, 1)
            dve.wait_ge(s_tabT, 1)
            dve.tensor_copy(slots[:], bk(AC, 0, P)).then_inc(s_slots, 1)

            def rows_T(e, j):
                dve.wait_ge(s_xTp, e + BASE + 1)
                dve.wait_ge(s_gu, e + BASE + 1 - 2)
                dve.tensor_copy(xT[j % 2][:], bk(MX[j % 2]).rearrange("p (c k) -> p c k", c=DC)).then_inc(s_xT, 1)

            def hidden(e, j):
                dve.wait_ge(s_sg, e + BASE + 1)
                dve.wait_ge(s_yp, e + BASE + 1 - 2)
                dve.tensor_tensor(hh[j % 2][0:F, :], bank[0:F, ST[j % 2], CAP:2 * CAP], sg[j % 2][0:F, :], ALU.mult
                                  ).then_inc(s_h, 1)

            dve.sem_inc(s_xT, BASE)
            dve.sem_inc(s_h, BASE)
            rows_T(0, 0)
            rows_T(1, 1)
            hidden(0, 0)
            with dve.Fori(0, E // RING - 1) as i:
                for j in range(RING):
                    e = i * RING + j
                    rows_T(e + 2, (j + 2) % RING)
                    hidden(e + 1, (j + 1) % RING)
            for e in range(E - RING, E):
                if e + 2 < E:
                    rows_T(e + 2, (e + 2) % RING)
                if e + 1 < E:
                    hidden(e + 1, (e + 1) % RING)

            def combine(b):
                for t in range(JT * b, JT * b + JT):
                    dve.wait_ge(s_yg[t % 2], 16 * TOPK * (t // 2 + 1))
                    for k in range(TOPK):
                        dve.scalar_tensor_tensor(x[:, t, :], yg[t % 2][:, k, :], wts[:, t, k:k + 1], x[:, t, :],
                                                 ALU.mult, ALU.add).then_inc(s_comb, 1)
                        dve.wait_ge(s_comb, TOPK * t + k + 1)

            def ffn(b):
                for hc in range(HC):
                    m = HC * b + hc
                    n = pd.next()
                    dve.wait_ge(s_fsg, m + 1)
                    if m >= 2:
                        dve.wait_ge(s_fdn, m - 1)
                    dve.tensor_tensor(hh[m % 2][:], bk(PD[n % 2], T, 2 * T), sg[m % 2][:], ALU.mult
                                      ).then_inc(s_pdf, 1)
                    dve.wait_ge(s_pdf, n + 1)
                    dve.engine_nop().then_inc(s_fh, 1)
                dve.wait_ge(s_fdn, HC * (b + 1))
                dve.tensor_tensor(x[:, tiles(b), :], bk(AC).rearrange("p (j d) -> p j d", j=JT), x[:, tiles(b), :],
                                  ALU.add).then_inc(s_fadd, 1)

            for s, g, attends, maxes, projects in steps(1):
                if s == 0:
                    combine(0)
                    combine(1)
                    combine(2)
                    combine(3)
                if attends:
                    attend(1, s - 2, g - 2)
                if maxes:
                    maxima(1, g - 1)
                if attends:
                    dve.wait_ge(s_fadd, s - 1)
                    output(s - 2, g - 2)
                if maxes:
                    negate(1, g - 1)
                    split_maxima(g - 1)
                if projects:
                    moments(1, s)
                    normalise(1, s)
                    project(g)
                    ffn(s)


def _pa_uses():
    n, uses = B, []
    for L in range(LAYERS):
        for s in range(STEPS):
            if s >= 2:
                n += 1
                uses.append(n)
            if s < B:
                n += 1 + L
    return uses


PA_USES = _pa_uses()


_OUT = ((B, T, D), "float32")


def kernel(**inputs):
    import numpy as np
    import concourse.bacc as bacc
    from concourse.bass_utils import run_bass_kernel_spmd

    a = {name: np.asarray(v) for name, v in inputs.items()}

    def expert_in(w):
        return np.ascontiguousarray(w.transpose(0, 2, 1).reshape(E, DC, P, F).transpose(0, 2, 1, 3))

    laid = {
        "x_in": a["L0_attn_x"],
        "wq0": a["L0_attn_Wq"], "wk0": a["L0_attn_Wk"], "wv0": a["L0_attn_Wv"], "wo0": a["L0_attn_Wo"],
        "gate_w": a["L0_ffn_gate_w"].T,
        "e_gate": expert_in(a["L0_ffn_w_gate"]), "e_up": expert_in(a["L0_ffn_w_up"]),
        "e_down": a["L0_ffn_w_down"].transpose(0, 2, 1),
        "wq1": a["L1_attn_Wq"].T, "wk1": a["L1_attn_Wk"].T, "wv1": a["L1_attn_Wv"].T, "wo1": a["L1_attn_Wo"].T,
        "f_gate": a["L1_ffn_w_gate"].T, "f_up": a["L1_ffn_w_up"].T, "f_down": a["L1_ffn_w_down"].T,
    }
    nc = bacc.Bacc("TRN2", target_bir_lowering=False, num_devices=1)
    arrays, args = {}, []
    for name, v in laid.items():
        v = np.ascontiguousarray(v)
        arrays[name] = v
        args.append(nc.dram_tensor(name, v.shape, mybir.dt.from_np(v.dtype), kind="ExternalInput").ap())
    shape, dtype = _OUT
    args.append(nc.dram_tensor("out", shape, mybir.dt.from_np(np.dtype(dtype)), kind="ExternalOutput").ap())
    build(nc, *args)
    return run_bass_kernel_spmd(nc, [arrays], core_ids=[0]).results[0]["out"]
```

```python
from contextlib import ExitStack

import concourse.bass as bass
from concourse import mybir

F32 = mybir.dt.float32
BF16 = mybir.dt.bfloat16
I32 = mybir.dt.int32
U32 = mybir.dt.uint32
ALU = mybir.AluOpType
ACT = mybir.ActivationFunctionType
AX = mybir.AxisListType

P = 128
B, T, D = 4, 256, 256
H, DH = 16, 16
JT = T // P
NT = B * JT
DC = D // P
E, TOPK, F = 64, 8, 96
CAP = 2 * (B * T * TOPK) // E
SC = CAP // P
HID = 1024
HC = HID // P
FFN_CHUNKS = (5, 6, 6, 5, 5, 5)
LAYERS = 2
SCALE = (1.0 / T ** 0.5, 1.0 / DH ** 0.5)
EPS = 1e-5
NEG = -1e30
LOW = -3e38
V1 = DH + 1
PARTS_Q = ((0, 1, 0), (1, 1, 0), (2, 1, 0), (3, 1, 1), (4, 1, 1), (5, 1, 2))
PARTS_K = ((0, 3, 0), (3, 2, 0), (5, 1, 0))
KS = 6 * DH
STACK_DMAS = len(PARTS_Q) + len(PARTS_K)
KM = KS + 3
NOWHERE = 1 << 16
RING = 4
BASE = 4
UNITS = 12
SLOTS = UNITS + 2


class Turns:

    def __init__(self):
        self.n = 0

    def next(self):
        self.n += 1
        return self.n - 1


def build(nc, x_in, wq0, wk0, wv0, wo0, gate_w, e_gate, e_up, e_down, wq1, wk1, wv1, wo1, f_gate, f_up, f_down, out):
    with ExitStack() as ctx:
        def sb(name, shape, dt=F32):
            return ctx.enter_context(nc.sbuf_tensor(name, shape, dt))

        def sem(name):
            return ctx.enter_context(nc.semaphore(name))

        def dram(name, shape, dt):
            return nc.dram_tensor(name, shape, dt, kind="Internal").ap()

        qk_dram = dram("qk_parts", [LAYERS * B, 2, 3, D, T], BF16)
        xn_dram = dram("xn_rows", [B * T, D], F32)
        table_dram = dram("slot_table", [E * CAP, 1], I32)
        y_dram = dram("expert_rows", [E * CAP, D], F32)

        x = sb("x", [P, NT, D])
        xn = sb("xn", [P, NT, D])
        xnT = sb("xnT", [P, DC, B * T])
        w_attn = [sb(f"w_attn{n}", [P, DC, D]) for n in range(8)]
        gwT = sb("gwT", [P, DC, E])
        wg1 = sb("wg1", [P, DC, HID])
        wu1 = sb("wu1", [P, DC, HID])
        wd1 = sb("wd1", [P, HC, D])
        identf = sb("identf", [P, P])
        later_f = sb("later_f", [P, P])
        ones_f = sb("ones_f", [P, P])
        identb = sb("identb", [P, P], BF16)
        mask_q = sb("mask_q", [P, P], BF16)
        mask_k = sb("mask_k", [P, P], BF16)
        earlier_b = sb("earlier_b", [P, P], BF16)
        ones_b = sb("ones_b", [P, P], BF16)
        floor = sb("floor", [P, LAYERS * JT])
        eps = sb("eps", [P, 1])
        e_idx = sb("e_idx", [P, E])
        e_base = sb("e_base", [P, E])
        tok_id = sb("tok_id", [P, NT], I32)
        nowhere = sb("nowhere", [P, P], I32)
        stats = sb("stats", [P, NT, 6])
        mv = sb("mv", [P, NT, 2])
        std = sb("std", [P, NT])
        rstd = sb("rstd", [P, NT])
        parts = [sb(f"parts{n}", [P, 3, DC, T], BF16) for n in range(2)]
        rest = [sb(f"rest{n}", [P, DC, T]) for n in range(2)]
        qs = [sb(f"qs{n}", [P, H, T], BF16) for n in range(2)]
        ks = [sb(f"ks{n}", [P, H, T], BF16) for n in range(2)]
        v1 = sb("v1", [P, NT * H, V1])
        mx = sb("mx", [P, JT, H])
        nm = sb("nm", [P, JT, P])
        nmc = sb("nmc", [P, JT, H])
        expn = [sb(f"expn{n}", [P, JT, H]) for n in range(2)]
        nms = sb("nms", [H, 3, T], BF16)
        nmr = sb("nmr", [H, T])
        nmr2 = sb("nmr2", [H, T])
        p0 = sb("p0", [P, H, T])
        p1 = sb("p1", [P, H, P])
        num = sb("num", [P, H, V1])
        rec = sb("rec", [P, H])
        attn = sb("attn", [P, JT, D])
        attnT = sb("attnT", [P, DC, T])
        rmax = sb("rmax", [P, NT])
        rsum = sb("rsum", [P, NT])
        rrec = sb("rrec", [P, NT])
        prob = sb("prob", [P, NT, E])
        rep = sb("rep", [P, NT, E])
        dest = sb("dest", [P, NT, E])
        top = sb("top", [P, NT, TOPK])
        topi = sb("topi", [P, NT, TOPK], U32)
        topf = sb("topf", [P, NT, TOPK])
        chosen = sb("chosen", [P, NT, E], BF16)
        destk = sb("destk", [P, NT, TOPK])
        desti = sb("desti", [P, NT, TOPK], I32)
        wts = sb("wts", [P, NT, TOPK])
        tab_i = sb("tab_i", [P, P], I32)
        tab_f = sb("tab_f", [P, P])
        slots = sb("slots", [P, P], I32)
        wgu = [sb(f"wgu{n}", [P, 2, DC, F]) for n in range(RING)]
        wdn = [sb(f"wdn{n}", [F, D]) for n in range(RING)]
        xg_all = sb("xg", [P, RING, SC, D])
        xg = [xg_all[:, n] for n in range(RING)]
        xT = [sb(f"xT{n}", [P, DC, CAP]) for n in range(2)]
        sg = [sb(f"sg{n}", [P, CAP]) for n in range(2)]
        hh = [sb(f"hh{n}", [P, CAP]) for n in range(2)]
        ysb_all = sb("ysb", [P, RING, SC, D])
        ysb = [ysb_all[:, n] for n in range(RING)]
        yg = [tile[:].rearrange("p r c d -> p (r c) d") for tile in (xg_all, ysb_all)]

        bank = ctx.enter_context(nc.psum_tensor("bank", [P, 8, 512], F32))
        MX, ST, PD = ((0, 6), (0,)), ((1, 7), (1,)), ((2, 3), (2,))
        PA, PV, GU, AC = 4, 5, (3, 6), 7
        EXT, EGU, EY = (0, 1), (2, 3), (4, 5)

        def bk(n, lo=0, hi=512):
            return bank[:, n, lo:hi]

        s_x = [sem(f"x_in{b}") for b in range(B)]
        s_w = [sem(f"w_in{n}") for n in range(12)]
        s_const = sem("const_ready")
        s_now = sem("nowhere_ready")
        s_set = sem("tiles_set")
        s_c0 = sem("const_zeroed")
        s_tab0 = sem("table_filled")
        s_stat = sem("stats_done")
        s_mv = sem("moments_done")
        s_std = sem("std_done")
        s_rstd = sem("rstd_done")
        s_xn = sem("xn_done")
        s_xnst = sem("xn_stored")
        s_pa = sem("pa_full")
        s_paf = sem("pa_drained")
        s_pd = sem("pd_full")
        s_pdf = sem("pd_drained")
        s_mxf = sem("max_bank_full")
        s_mxd = sem("max_bank_drained")
        s_st = sem("score_bank_full")
        s_exp = sem("exp_done")
        s_hi = sem("hi_done")
        s_rest = sem("rest_done")
        s_mid = sem("mid_done")
        s_lo = sem("lo_done")
        s_qkst = [sem(f"qk_stored{n}") for n in range(2)]
        s_stack = [sem(f"stack_in{n}") for n in range(2)]
        s_nm = sem("neg_max_done")
        s_nmc = sem("neg_max_clamped")
        s_nms = sem("neg_max_parts_done")
        s_nmrow = sem("neg_max_rows_in")
        s_nch = sem("neg_max_chain")
        s_expn = sem("exp_neg_max_done")
        s_ach = sem("attend_chain")
        s_attn = sem("attn_done")
        s_oadd = sem("attn_added")
        s_lg = sem("logits_done")
        s_rch = sem("router_chain")
        s_rsh = sem("router_shifted")
        s_rexp = sem("router_exp_done")
        s_chosen = sem("chosen_done")
        s_pos = sem("positions_done")
        s_dest = sem("dest_done")
        s_scat = sem("scattered")
        s_tab = sem("table_read")
        s_tabf = sem("table_float")
        s_tabT = sem("table_turned")
        s_slots = sem("slots_done")
        s_wts = [sem(f"expert_w{n}") for n in range(RING)]
        s_xg = [sem(f"expert_x{n}") for n in range(RING)]
        s_yst = [sem(f"expert_y{n}") for n in range(RING)]
        s_xTp = sem("expert_xT_psum")
        s_xT = sem("expert_xT")
        s_gu = sem("expert_gu")
        s_sg = sem("expert_silu")
        s_h = sem("expert_h")
        s_yp = sem("expert_y_psum")
        s_y = sem("expert_y")
        s_yg = [sem(f"rows_back{n}") for n in range(2)]
        s_comb = sem("combine_chain")
        s_fsg = sem("ffn_silu")
        s_fh = sem("ffn_h")
        s_pv = sem("pv_full")
        s_pvf = sem("pv_drained")
        s_fgu = sem("ffn_gate_up")
        s_ft = sem("ffn_silu_chain")
        s_fdn = sem("ffn_down")
        s_fadd = sem("ffn_added")
        s_out = sem("out_stored")

        block = ctx.enter_context(nc.Block())

        def tiles(b):
            return slice(JT * b, JT * b + JT)

        def schedule(L):
            ffn_at, chunk = {}, 0
            if L == 1:
                for s, count in enumerate(FFN_CHUNKS):
                    for i in range(count):
                        ffn_at[s, 2 + i * (SLOTS - 2) // count] = chunk
                        chunk += 1
            last = None
            for s in range(B + 3):
                p, m, a, o = s, s - 1, s - 2, s - 3
                for slot in range(SLOTS):
                    if p < B:
                        if slot == 0:
                            yield "part_hi", p, 0
                        if slot == 1:
                            yield "value", p, 0
                            yield "part_lo", p, 0
                            yield "part_hi", p, 1
                        if slot == 2:
                            yield "part_lo", p, 1
                            if L == 0 and p == 0:
                                yield "router", p, 0
                    if L == 0 and s == 1 and slot <= TOPK:
                        yield "destination", 0, slot
                    if 0 <= m < B and slot < UNITS:
                        yield "max", m, slot
                    if 0 <= a < B and slot >= 2:
                        yield "score", a, slot - 2
                    if 0 <= o < B and slot == 1:
                        yield "out_turn", o, 0
                    if 0 <= o < B and slot == 3:
                        yield "out_proj", o, 0
                    if (s, slot) in ffn_at:
                        yield "ffn_in", ffn_at[s, slot] // HC, ffn_at[s, slot]
                        if last is not None:
                            yield "ffn_hidden", last // HC, last
                            yield "ffn_down", last // HC, last
                        last = ffn_at[s, slot]
                    if L == 1 and p + 1 < B and 4 <= slot < 12:
                        yield "combine", p + 1, 2 * (slot - 4)
                        yield "combine", p + 1, 2 * (slot - 4) + 1
                    if L == 1 and p + 1 < B and slot == 12:
                        yield "norm", p + 1, 0
                    if 0 <= a < B and slot == 3 and L == 0:
                        yield "hidden_sum", a, 0
                    if 0 <= a < B and 4 <= slot < 12:
                        yield "pv0", a, slot - 4
                    if 0 <= m < B and slot == UNITS:
                        yield "negate", m, 0
                if 0 <= a < B and L == 0:
                    yield "hidden_sum", a, 1
                for quad in range(4):
                    if 0 <= a < B:
                        yield "pv1", a, quad
                    if quad == 0 and 0 <= m < B:
                        yield "turn_max", m, 0
                    if quad == 1 and L == 1 and p + 1 < B:
                        yield "turn", p + 1, 0
            if L == 1:
                yield "ffn_hidden", last // HC, last
                yield "ffn_down", last // HC, last

        def unit_heads(u):
            if u < 8:
                return range(2 * u, 2 * u + 2), T
            return range(4 * (u - 8), 4 * (u - 8) + 4), P

        CONSTS = 4 + 6 + 1 + 3
        SETS = 4 + RING

        @block.sync
        def _(sp):
            xv = x_in.rearrange("b (j p) d -> p b j d", p=P)
            for b in range(B):
                sp.dma_start(x[:, tiles(b), :], xv[:, b]).then_inc(s_x[b], 16)
            for n, w in enumerate((wq0, wk0, wv0, wo0)):
                sp.dma_start(w_attn[n][:], w.rearrange("(c p) n -> p c n", p=P)).then_inc(s_w[n], 16)
            sp.dma_start(gwT[:], gate_w.rearrange("(c p) n -> p c n", p=P)).then_inc(s_w[8], 16)
            sp.wait_ge(s_now, 1)
            sp.dma_start(table_dram.rearrange("(r c) one -> r (c one)", c=P), nowhere[:]).then_inc(s_tab0, 16)
            sp.wait_ge(s_xn, NT)
            sp.dma_start(xn_dram.rearrange("(t p) d -> p t d", p=P), xn[:]).then_inc(s_xnst, 16)

            def expert_weights(e, j):
                sp.dma_start(wgu[j][:, 0], e_gate[e]).then_inc(s_wts[j], 16)
                sp.dma_start(wgu[j][:, 1], e_up[e]).then_inc(s_wts[j], 16)
                sp.dma_start(wdn[j][:], e_down[e]).then_inc(s_wts[j], 16)

            def attention_moves(L):
                for what, b, i in schedule(L):
                    g = B * L + b
                    if what == "turn_max":
                        sp.wait_ge(s_nms, g + 1)
                        for r in range(3):
                            sp.dma_start(qs[g % 2][KS + r:KS + r + 1, :, :], nms[:, r, :]).then_inc(s_nmrow, 16)
                    if what == "part_lo":
                        stack, order = ((qs, PARTS_Q), (ks, PARTS_K))[i]
                        sp.wait_ge(s_lo, 2 * g + i + 1)
                        sp.dma_start(qk_dram[g, i].rearrange("s (m p) t -> p (s m) t", p=P),
                                     parts[i][:].rearrange("p s m t -> p (s m) t")).then_inc(s_qkst[i], 16)
                        sp.wait_ge(s_qkst[i], 16 * (g + 1))
                        if g >= 2:
                            sp.wait_ge(s_st, UNITS * (g - 1))
                        for first, count, part in order:
                            sp.dma_start(stack[g % 2][first * DH:(first + count) * DH].rearrange("p h t -> p (h t)"),
                                         qk_dram[g, i, part:part + count].rearrange("s (d h) t -> (s d) (h t)", d=DH)
                                         ).then_inc(s_stack[g % 2], 16)

            attention_moves(0)
            for n, w in enumerate((wq1, wk1, wv1, wo1)):
                sp.dma_start(w_attn[4 + n][:], w.rearrange("(c p) n -> p c n", p=P)).then_inc(s_w[4 + n], 16)
            for n, (tile, w) in enumerate(((wg1, f_gate), (wu1, f_up), (wd1, f_down))):
                sp.dma_start(tile[:], w.rearrange("(c p) n -> p c n", p=P)).then_inc(s_w[9 + n], 16)
            for j in range(RING):
                expert_weights(j, j)
            sp.wait_ge(s_scat, 16 * NT * TOPK)
            sp.dma_start(tab_i[:], table_dram.rearrange("(r c) one -> r (c one)", c=P)).then_inc(s_tab, 16)

            def store_rows(e, j):
                sp.wait_ge(s_y, BASE + 1 + e)
                sp.dma_start(y_dram.rearrange("(e c p) d -> e p c d", e=E, p=P)[e], ysb[j]).then_inc(s_yst[j], 16)

            with sp.Fori(0, E // RING - 1) as i:
                for j in range(RING):
                    store_rows(i * RING + j, j)
                    expert_weights(i * RING + j + RING, j)
            for j in range(RING):
                store_rows(E - RING + j, j)
            attention_moves(1)
            for b in range(B):
                sp.wait_ge(s_oadd, B + b + 1)
                sp.wait_ge(s_fadd, b + 1)
                sp.dma_start(out.rearrange("b (j p) d -> p b j d", p=P)[:, b], x[:, tiles(b), :]).then_inc(s_out, 16)
            sp.wait_ge(s_out, 16 * B)

        @block.gpsimd
        def _(pool):
            pool.memset(nowhere[:], NOWHERE).then_inc(s_now, 1)
            for tile in (identf, later_f, identb, mask_q, mask_k, earlier_b):
                pool.memset(tile[:], 0.0).then_inc(s_c0, 1)
            pool.memset(floor[:, 0:JT], 0.0).then_inc(s_c0, 1)
            pool.memset(ones_f[:], 1.0).then_inc(s_const, 1)
            pool.memset(ones_b[:], 1.0).then_inc(s_const, 1)
            pool.memset(floor[:, JT:], LOW).then_inc(s_const, 1)
            pool.memset(eps[:], EPS).then_inc(s_const, 1)
            pool.wait_ge(s_c0, 7)
            diag = dict(compare_op=ALU.not_equal, pattern=[[-1, P]], base=0, channel_multiplier=1)
            row_ge = dict(compare_op=ALU.is_ge, pattern=[[-1, P]], base=0, channel_multiplier=1)
            col_ge = dict(compare_op=ALU.is_ge, pattern=[[1, P]], base=0, channel_multiplier=-1)
            for tile, where, fill in ((identf, diag, 1.0), (identb, diag, 1.0), (later_f, col_ge, 1.0),
                                      (mask_q, row_ge, NEG), (mask_k, col_ge, NEG), (earlier_b, row_ge, 1.0)):
                pool.affine_select(out=tile[:], in_=tile[:], fill=fill, **where).then_inc(s_const, 1)
            pool.affine_select(out=floor[:, JT - 1:JT], in_=floor[:, JT - 1:JT], compare_op=ALU.not_equal, fill=LOW,
                               pattern=[[0, 1]], base=-(P - 1), channel_multiplier=1).then_inc(s_const, 1)
            pool.iota(e_idx[:], [[1, E]], base=0, channel_multiplier=0, allow_small_or_imprecise_dtypes=True
                      ).then_inc(s_const, 1)
            pool.iota(e_base[:], [[CAP, E]], base=0, channel_multiplier=0, allow_small_or_imprecise_dtypes=True
                      ).then_inc(s_const, 1)
            pool.iota(tok_id[:], [[P, NT]], base=0, channel_multiplier=1).then_inc(s_const, 1)

            pool.wait_ge(s_set, SETS)
            pool.wait_ge(s_dest, 1)
            pool.wait_ge(s_tab0, 16)
            for t in range(NT):
                for k in range(TOPK):
                    pool.indirect_dma_start(table_dram, bass.IndirectOffsetOnAxis(desti[:, t, k:k + 1], 0),
                                            tok_id[:, t:t + 1], None, bounds_check=E * CAP - 1, oob_is_err=False
                                            ).then_inc(s_scat, 16)
            pool.wait_ge(s_slots, 1)
            pool.wait_ge(s_xnst, 16)
            for e in range(E):
                if e >= RING:
                    pool.wait_ge(s_xTp, BASE + 1 + e - RING)
                for c in range(SC):
                    pool.indirect_dma_start(xg[e % RING][:, c, :], None, xn_dram,
                                            bass.IndirectOffsetOnAxis(slots[:, e * SC + c:e * SC + c + 1], 0),
                                            bounds_check=B * T - 1, oob_is_err=False).then_inc(s_xg[e % RING], 16)
            for j in range(RING):
                pool.wait_ge(s_yst[j], 16 * (E // RING))
            for t in range(NT):
                if t >= 2:
                    pool.wait_ge(s_comb, TOPK * (t - 1))
                for k in range(TOPK):
                    pool.indirect_dma_start(yg[t % 2][:, k, :], None, y_dram,
                                            bass.IndirectOffsetOnAxis(desti[:, t, k:k + 1], 0),
                                            bounds_check=E * CAP - 1, oob_is_err=False).then_inc(s_yg[t % 2], 16)

        @block.tensor
        def _(pe):
            pd, pa, mt, stt, pv = Turns(), Turns(), Turns(), Turns(), Turns()

            turned, out_turned = {}, {}

            def take_pd(L):
                n = pd.next()
                if n >= len(PD[L]):
                    pe.wait_ge(s_pdf, n + 1 - len(PD[L]))
                return PD[L][n % len(PD[L])]

            def take_pa():
                n = pa.next()
                if n >= 1:
                    pe.wait_ge(s_paf, n)
                return PA

            def turn(L, b):
                pe.wait_ge(s_xn, NT * L + JT * (b + 1))
                bn = take_pa()
                for c in range(DC):
                    for j in range(JT):
                        last = pe.transpose(bk(bn, c * T + j * P, c * T + (j + 1) * P),
                                            xn[:, JT * b + j, c * P:(c + 1) * P], identf[:])
                last.then_inc(s_pa, 1)

            def part_hi(L, b, n):
                bn = take_pd(L)
                if b == 0:
                    pe.wait_ge(s_w[4 * L + n], 16)
                for m in range(DC):
                    for c in range(DC):
                        last = pe.matmul(bk(bn, m * T, (m + 1) * T), w_attn[4 * L + n][:, c, m * P:(m + 1) * P],
                                         xnT[:, c, b * T:(b + 1) * T], start=c == 0, stop=c == DC - 1)
                last.then_inc(s_pd, 1)

            def value(L, b):
                bn = take_pa()
                if b == 0:
                    pe.wait_ge(s_w[4 * L + 2], 16)
                for j in range(JT):
                    for c in range(DC):
                        last = pe.matmul(bk(bn, j * D, (j + 1) * D),
                                         xnT[:, c, b * T + j * P:b * T + (j + 1) * P], w_attn[4 * L + 2][:, c, :],
                                         start=c == 0, stop=c == DC - 1)
                last.then_inc(s_pa, 1)

            def maximum(L, g, u):
                if u == 0:
                    pe.wait_ge(s_stack[g % 2], 16 * STACK_DMAS * (g // 2 + 1))
                n = mt.next()
                ring = MX[L]
                if n >= len(ring):
                    pe.wait_ge(s_mxd, n + 1 - len(ring))
                bn = ring[n % len(ring)]
                heads, w = unit_heads(u)
                q0 = T - P if w == T else 0
                for i, h in enumerate(heads):
                    o = i * w
                    pe.matmul(bk(bn, o, o + w), qs[g % 2][0:KS, h, q0:q0 + P], ks[g % 2][0:KS, h, 0:w],
                              start=True, stop=False)
                    last = pe.matmul(bk(bn, o + w - P, o + w), identb[:], mask_q[:], start=False, stop=True)
                last.then_inc(s_mxf, 1)

            def score(L, g, u):
                if u == 0:
                    pe.wait_ge(s_nmrow, 48 * (g + 1))
                n = stt.next()
                ring = ST[L]
                if n >= len(ring):
                    pe.wait_ge(s_exp, n + 1 - len(ring))
                bn = ring[n % len(ring)]
                heads, w = unit_heads(u)
                k0 = 0 if w == T else P
                for i, h in enumerate(heads):
                    o = i * w
                    pe.matmul(bk(bn, o, o + w), ks[g % 2][0:KM, h, k0:k0 + P], qs[g % 2][0:KM, h, T - w:T],
                              start=True, stop=False)
                    last = pe.matmul(bk(bn, o, o + P), identb[:], mask_k[:], start=False, stop=True)
                last.then_inc(s_st, 1)

            def hidden_sum(b, j):
                bn = take_pd(0)
                last = pe.matmul(bk(bn, 0, H * V1), later_f[:], v1[:, (JT * b + j) * H:(JT * b + j + 1) * H, :],
                                 start=True, stop=j == JT - 1)
                if j == 0:
                    last = pe.matmul(bk(bn, 0, H * V1), ones_f[:], v1[:, (JT * b + 1) * H:(JT * b + 2) * H, :],
                                     start=False, stop=True)
                last.then_inc(s_pd, 1)

            def pv0(b, g, i):
                if i == 0:
                    n = pv.next()
                    if n >= 1:
                        pe.wait_ge(s_pvf, n)
                pe.wait_ge(s_exp, UNITS * g + i + 1)
                for h in (2 * i, 2 * i + 1):
                    last = pe.matmul(bk(PV, h * V1, (h + 1) * V1), p0[:, h, 0:P], v1[:, JT * b * H + h, :],
                                     start=True, stop=True)
                if i == 7:
                    last.then_inc(s_pv, 1)

            def pv1(b, g, quad):
                if quad == 0:
                    n = pv.next()
                    pe.wait_ge(s_pvf, n)
                pe.wait_ge(s_exp, UNITS * g + 8 + quad + 1)
                for h in range(4 * quad, 4 * quad + 4):
                    o = bk(PV, h * V1, (h + 1) * V1)
                    pe.matmul(o, p0[:, h, P:T], v1[:, JT * b * H + h, :], start=True, stop=False)
                    last = pe.matmul(o, p1[:, h, :], v1[:, (JT * b + 1) * H + h, :], start=False, stop=True)
                if quad == 3:
                    last.then_inc(s_pv, 1)

            def out_turn(g):
                pe.wait_ge(s_attn, JT * (g + 1))
                bn = take_pa()
                for c in range(DC):
                    for j in range(JT):
                        last = pe.transpose(bk(bn, c * T + j * P, c * T + (j + 1) * P),
                                            attn[:, j, c * P:(c + 1) * P], identf[:])
                last.then_inc(s_pa, 1)
                out_turned[g] = pa.n

            def out_proj(L, b, g):
                pe.wait_ge(s_paf, out_turned[g])
                bn = take_pd(L)
                if b == 0:
                    pe.wait_ge(s_w[4 * L + 3], 16)
                for j in range(JT):
                    for c in range(DC):
                        last = pe.matmul(bk(bn, j * D, (j + 1) * D), attnT[:, c, j * P:(j + 1) * P],
                                         w_attn[4 * L + 3][:, c, :], start=c == 0, stop=c == DC - 1)
                last.then_inc(s_pd, 1)

            def turn_maxima(L, g):
                pe.wait_ge(s_nm, g + 1)
                bn = take_pd(L)
                for j in range(JT):
                    last = pe.transpose(bk(bn, j * P, (j + 1) * P), nm[:, j, :], identf[:])
                last.then_inc(s_pd, 1)

            def ffn_in(b, m):
                hc = m % HC
                if m == 0:
                    for n in range(3):
                        pe.wait_ge(s_w[9 + n], 16)
                if m >= 2:
                    pe.wait_ge(s_fh, m - 1)
                for n, w in enumerate((wg1, wu1)):
                    for c in range(DC):
                        last = pe.matmul(bk(GU[m % 2], n * T, (n + 1) * T), w[:, c, hc * P:(hc + 1) * P],
                                         xnT[:, c, b * T:(b + 1) * T], start=c == 0, stop=c == DC - 1)
                last.then_inc(s_fgu, 1)

            def ffn_down(b, m):
                hc = m % HC
                pe.wait_ge(s_fh, m + 1)
                if hc == 0 and b > 0:
                    pe.wait_ge(s_fadd, b)
                for j in range(JT):
                    last = pe.matmul(bk(AC, j * D, (j + 1) * D), hh[m % 2][:, j * P:(j + 1) * P], wd1[:, hc, :],
                                     start=hc == 0 and j == 0, stop=hc == HC - 1, skip_group_check=True)
                last.then_inc(s_fdn, 1)

            def layer(L):
                for what, b, i in schedule(L):
                    g = B * L + b
                    if what == "turn":
                        turn(L, b)
                        turned[g] = pa.n
                    if what == "part_hi":
                        if i == 0:
                            pe.wait_ge(s_paf, turned[g])
                        part_hi(L, b, i)
                    if what == "router":
                        logits()
                        positions()
                    if what == "value":
                        value(L, b)
                    if what == "max":
                        maximum(L, g, i)
                    if what == "score":
                        score(L, g, i)
                    if what == "hidden_sum":
                        hidden_sum(b, i)
                    if what == "pv0":
                        pv0(b, g, i)
                    if what == "pv1":
                        pv1(b, g, i)
                    if what == "turn_max":
                        turn_maxima(L, g)
                    if what == "out_turn":
                        out_turn(g)
                    if what == "out_proj":
                        out_proj(L, b, g)
                    if what == "ffn_in":
                        ffn_in(b, i)
                    if what == "ffn_down":
                        ffn_down(b, i)

            pe.wait_ge(s_const, CONSTS)
            for b in range(B):
                turn(0, b)
                turned[b] = pa.n

            def logits():
                pe.wait_ge(s_w[8], 16)
                pe.wait_ge(s_paf, turned[B - 1])
                for t in range(NT):
                    for c in range(DC):
                        last = pe.matmul(bk(AC, t * E, (t + 1) * E), xnT[:, c, t * P:(t + 1) * P], gwT[:, c, :],
                                         start=c == 0, stop=c == DC - 1)
                last.then_inc(s_lg, 1)

            def positions():
                pe.wait_ge(s_chosen, 1)
                for t in range(NT):
                    o = bk(AC, t * E, (t + 1) * E)
                    for before in range(t):
                        pe.matmul(o, ones_b[:], chosen[:, before, :], start=before == 0, stop=False)
                    last = pe.matmul(o, earlier_b[:], chosen[:, t, :], start=t == 0, stop=True)
                last.then_inc(s_pos, 1)

            pe.wait_ge(s_set, SETS)
            layer(0)

            pe.wait_ge(s_tabf, 1)
            pe.transpose(bk(AC, 0, P), tab_f[:], identf[:]).then_inc(s_tabT, 1)
            pe.wait_ge(s_mxd, mt.n)
            pe.wait_ge(s_exp, stt.n)
            pe.wait_ge(s_pdf, pd.n)
            pe.wait_ge(s_pvf, pv.n)
            pe.wait_ge(s_paf, pa.n)

            def e_turn(e, j, i):
                pe.wait_ge(s_xg[j], 16 * SC * (i + 1))
                pe.wait_ge(s_xT, e + BASE + 1 - 2)
                for c in range(DC):
                    for k in range(SC):
                        last = pe.transpose(bk(EXT[j % 2], c * CAP + k * P, c * CAP + (k + 1) * P),
                                            xg[j][:, k, c * P:(c + 1) * P], identf[:])
                last.then_inc(s_xTp, 1)

            def e_gate_up(e, j, i):
                pe.wait_ge(s_xT, e + BASE + 1)
                pe.wait_ge(s_wts[j], 48 * (i + 1))
                pe.wait_ge(s_h, e + BASE + 1 - 2)
                for n in range(2):
                    for c in range(DC):
                        last = pe.matmul(bank[0:F, EGU[j % 2], n * CAP:(n + 1) * CAP], wgu[j][:, n, c, :],
                                         xT[j % 2][:, c, :], start=c == 0, stop=c == DC - 1)
                last.then_inc(s_gu, 1)

            def e_down_(e, j, i):
                pe.wait_ge(s_h, e + BASE + 1)
                pe.wait_ge(s_y, e + BASE + 1 - 2)
                for k in range(SC):
                    last = pe.matmul(bk(EY[j % 2], k * D, (k + 1) * D), hh[j % 2][0:F, k * P:(k + 1) * P], wdn[j][:],
                                     start=True, stop=True)
                last.then_inc(s_yp, 1)

            pe.sem_inc(s_xTp, BASE)
            pe.sem_inc(s_gu, BASE)
            pe.sem_inc(s_yp, BASE)
            e_turn(0, 0, 0)
            e_turn(1, 1, 0)
            e_gate_up(0, 0, 0)
            with pe.Fori(0, E // RING - 1) as i:
                for j in range(RING):
                    e = i * RING + j
                    e_turn(e + 2, (j + 2) % RING, i + (j + 2) // RING)
                    e_gate_up(e + 1, (j + 1) % RING, i + (j + 1) // RING)
                    e_down_(e, j, i)
            for e in range(E - RING, E):
                if e + 2 < E:
                    e_turn(e + 2, (e + 2) % RING, (e + 2) // RING)
                if e + 1 < E:
                    e_gate_up(e + 1, (e + 1) % RING, (e + 1) // RING)
                e_down_(e, e % RING, e // RING)
            pe.wait_ge(s_y, E + BASE)

            turn(1, 0)
            turned[B] = pa.n
            layer(1)

        @block.scalar
        def _(act):
            pd, pa, stt = Turns(), Turns(), Turns()

            def drain_pa(dst, src_shape):
                n = pa.next()
                act.wait_ge(s_pa, n + 1)
                act.activation(dst, bk(PA).rearrange("p (a b) -> p a b", a=src_shape), ACT.Copy).then_inc(s_paf, 1)

            def std_of(L, b):
                act.wait_ge(s_mv, NT * L + JT * (b + 1))
                act.activation(std[:, tiles(b)], mv[:, tiles(b), 1], ACT.Sqrt, bias=eps[:]).then_inc(s_std, 1)

            def exp_unit(L, g, u):
                n = stt.next()
                act.wait_ge(s_st, n + 1)
                if u == 0 and g > 0:
                    act.wait_ge(s_pv, JT * g)
                heads, w = unit_heads(u)
                dst = (p0 if w == T else p1)[:, heads[0]:heads[-1] + 1, :]
                act.activation(dst, bk(ST[L][n % len(ST[L])]).rearrange("p (a b) -> p a b", b=w), ACT.Exp,
                               scale=SCALE[L]).then_inc(s_exp, 1)

            def part_hi(L, g, i, n):
                act.wait_ge(s_pd, n + 1)
                if g > 0:
                    act.wait_ge(s_qkst[i], 16 * g)
                act.activation(parts[i][:, 0], bk(PD[L][n % len(PD[L])]).rearrange("p (m t) -> p m t", m=DC),
                               ACT.Copy).then_inc(s_hi, 1)

            def part_mid(g, i):
                act.wait_ge(s_rest, 2 * g + i + 1)
                act.activation(parts[i][:, 1], rest[i][:], ACT.Copy).then_inc(s_mid, 1)

            def value(b):
                n = pa.next()
                act.wait_ge(s_pa, n + 1)
                act.activation(v1[:, JT * b * H:JT * (b + 1) * H, 0:DH],
                               bk(PA).rearrange("p (a d) -> p a d", d=DH), ACT.Copy).then_inc(s_paf, 1)

            def out_turn(g):
                n = pa.next()
                act.wait_ge(s_pa, n + 1)
                act.wait_ge(s_oadd, g)
                act.activation(attnT[:], bk(PA).rearrange("p (a b) -> p a b", a=DC), ACT.Copy).then_inc(s_paf, 1)

            def layer(L):
                for what, b, i in schedule(L):
                    g = B * L + b
                    if what == "turn":
                        drain_pa(xnT[:, :, b * T:(b + 1) * T], DC)
                    if what == "part_hi":
                        part_hi(L, g, i, pd.next())
                    if what == "router":
                        act.wait_ge(s_rsh, 1)
                        act.activation(prob[:], rep[:], ACT.Exp).then_inc(s_rexp, 1)
                    if what == "part_lo":
                        part_mid(g, i)
                    if what == "value":
                        value(b)
                    if what == "score":
                        exp_unit(L, g, i)
                    if what == "negate" and L == 0:
                        act.wait_ge(s_nmc, g + 1)
                        act.activation(expn[g % 2][:], nmc[:], ACT.Exp, scale=SCALE[L]).then_inc(s_expn, 1)
                    if what in ("hidden_sum", "turn_max", "out_proj"):
                        pd.next()
                    if what == "out_turn":
                        out_turn(g)
                    if what == "ffn_in":
                        act.wait_ge(s_fgu, i + 1)
                        if i >= 2:
                            act.wait_ge(s_fh, i - 1)
                        act.activation(sg[i % 2][:], bk(GU[i % 2], 0, T), ACT.Tanh, scale=0.5).then_inc(s_fsg, 1)
                    if what == "norm":
                        std_of(L, b)

            act.wait_ge(s_const, CONSTS)
            for b in range(B):
                std_of(0, b)
            for b in range(B):
                drain_pa(xnT[:, :, b * T:(b + 1) * T], DC)
            act.wait_ge(s_set, SETS)
            layer(0)

            def silu(e, j):
                act.wait_ge(s_gu, e + BASE + 1)
                act.wait_ge(s_h, e + BASE + 1 - 2)
                act.activation(sg[j % 2][0:F, :], bank[0:F, EGU[j % 2], 0:CAP], ACT.Silu).then_inc(s_sg, 1)

            def rows_out(e, j, i):
                act.wait_ge(s_yp, e + BASE + 1)
                act.wait_ge(s_yst[j], 16 * i)
                act.activation(ysb[j], bk(EY[j % 2]).rearrange("p (c d) -> p c d", c=SC), ACT.Copy
                               ).then_inc(s_y, 1)

            act.sem_inc(s_sg, BASE)
            act.sem_inc(s_y, BASE)
            silu(0, 0)
            with act.Fori(0, E // RING - 1) as i:
                for j in range(RING):
                    silu(i * RING + j + 1, (j + 1) % RING)
                    rows_out(i * RING + j, j, i)
            for e in range(E - RING, E):
                if e + 1 < E:
                    silu(e + 1, (e + 1) % RING)
                rows_out(e, e % RING, e // RING)

            std_of(1, 0)
            drain_pa(xnT[:, :, 0:T], DC)
            layer(1)

        @block.vector
        def _(dve):
            pd, pa, mt, pv = Turns(), Turns(), Turns(), Turns()
            nch, ach, rch = Turns(), Turns(), Turns()

            def link(ins, s, turns):
                turns.next()
                ins.then_inc(s, 1)
                dve.wait_ge(s, turns.n)

            def moments(L, b):
                for t in range(JT * b, JT * b + JT):
                    dve.bn_stats(stats[:, t, :], x[:, t, :]).then_inc(s_stat, 1)
                dve.wait_ge(s_stat, NT * L + JT * (b + 1))
                for t in range(JT * b, JT * b + JT):
                    dve.bn_aggr(mv[:, t, :], stats[:, t, :]).then_inc(s_mv, 1)

            def normalise(L, b):
                dve.wait_ge(s_std, B * L + b + 1)
                dve.wait_ge(s_mv, NT * L + JT * (b + 1))
                dve.reciprocal(rstd[:, tiles(b)], std[:, tiles(b)]).then_inc(s_rstd, 1)
                dve.wait_ge(s_rstd, B * L + b + 1)
                for t in range(JT * b, JT * b + JT):
                    dve.tensor_scalar(xn[:, t, :], x[:, t, :], mv[:, t, 0:1], rstd[:, t:t + 1],
                                      ALU.subtract, ALU.mult).then_inc(s_xn, 1)

            def reduce_unit(L, g, u):
                if u == 0 and g > 0:
                    dve.wait_ge(s_nm, g)
                n = mt.next()
                heads, w = unit_heads(u)
                dve.wait_ge(s_mxf, n + 1)
                dve.reduce_max(mx[:, 1 if w == T else 0, heads[0]:heads[-1] + 1],
                               bk(MX[L][n % len(MX[L])]).rearrange("p (a b) -> p a b", b=w), AX.X).then_inc(s_mxd, 1)

            def negate(L, g):
                dve.wait_ge(s_mxd, UNITS * (g + 1))
                if L == 0 and g > 0:
                    dve.wait_ge(s_expn, g)
                for j in range(JT):
                    ins = dve.tensor_scalar(nm[:, j, 0:H], mx[:, j, :], floor[:, JT * L + j:JT * L + j + 1], -1.0,
                                            ALU.max, ALU.mult)
                ins.then_inc(s_nm, 1)
                if L == 0:
                    dve.wait_ge(s_nm, g + 1)
                    dve.tensor_scalar(nmc[:], nm[:, :, 0:H], 0.0, None, ALU.min).then_inc(s_nmc, 1)

            def split_maxima(L, g):
                n = pd.next()
                dve.wait_ge(s_pd, n + 1)
                if g > 0:
                    dve.wait_ge(s_nms, g)
                    dve.wait_ge(s_nmrow, 48 * g)
                src = bank[0:H, PD[L][n % len(PD[L])], 0:T]
                link(dve.tensor_copy(nms[:, 0, :], src), s_nch, nch)
                dve.tensor_tensor(nmr[:], src, nms[:, 0, :], ALU.subtract).then_inc(s_pdf, 1)
                dve.wait_ge(s_pdf, n + 1)
                link(dve.tensor_copy(nms[:, 1, :], nmr[:]), s_nch, nch)
                dve.tensor_tensor(nms[:, 2, :], nmr[:], nms[:, 1, :], ALU.subtract).then_inc(s_nms, 1)

            def hidden_sum(L, g, j):
                dve.wait_ge(s_expn, g + 1)
                n = pd.next()
                dve.wait_ge(s_pd, n + 1)
                if g > 0 or j > 0:
                    dve.wait_ge(s_attn, JT * g + j)
                dve.tensor_tensor(num[:], bk(PD[L][n % len(PD[L])], 0, H * V1).rearrange("p (h d) -> p h d", d=V1),
                                  expn[g % 2][:, j, :].unsqueeze(2).broadcast_to([P, H, V1]), ALU.mult
                                  ).then_inc(s_pdf, 1)
                dve.wait_ge(s_pdf, n + 1)

            def attended(L, g, j):
                n = pv.next()
                dve.wait_ge(s_pv, n + 1)
                src = bk(PV, 0, H * V1).rearrange("p (h d) -> p h d", d=V1)
                if L == 0:
                    dve.tensor_tensor(num[:], src, num[:], ALU.add).then_inc(s_pvf, 1)
                    dve.wait_ge(s_pvf, n + 1)
                    src = num[:]
                if JT * g + j > 0:
                    dve.wait_ge(s_attn, JT * g + j)
                link(dve.reciprocal(rec[:], src[:, :, DH]), s_ach, ach)
                if g > 0 and j == 0:
                    dve.wait_ge(s_oadd, g)
                dve.tensor_tensor(attn[:, j, :].rearrange("p (h d) -> p h d", d=DH), src[:, :, 0:DH],
                                  rec[:].unsqueeze(2).broadcast_to([P, H, DH]), ALU.mult).then_inc(s_attn, 1)
                if L == 1:
                    dve.wait_ge(s_attn, JT * g + j + 1)
                    dve.engine_nop().then_inc(s_pvf, 1)

            def output(L, b, g):
                n = pd.next()
                dve.wait_ge(s_pd, n + 1)
                dve.tensor_tensor(x[:, tiles(b), :], bk(PD[L][n % len(PD[L])]).rearrange("p (j d) -> p j d", j=JT),
                                  x[:, tiles(b), :], ALU.add).then_inc(s_pdf, 1)
                dve.wait_ge(s_pdf, n + 1)
                dve.engine_nop().then_inc(s_oadd, 1)

            def part_rest(L, g, i):
                n = pd.next()
                if g > 0:
                    dve.wait_ge(s_lo, 2 * (g - 1) + i + 1)
                dve.wait_ge(s_hi, 2 * g + i + 1)
                dve.tensor_tensor(rest[i][:], bk(PD[L][n % len(PD[L])]).rearrange("p (m t) -> p m t", m=DC),
                                  parts[i][:, 0], ALU.subtract).then_inc(s_pdf, 1)
                dve.wait_ge(s_pdf, n + 1)
                dve.engine_nop().then_inc(s_rest, 1)

            def part_lo(g, i):
                dve.wait_ge(s_mid, 2 * g + i + 1)
                dve.tensor_tensor(parts[i][:, 2], rest[i][:], parts[i][:, 1], ALU.subtract).then_inc(s_lo, 1)

            def router():
                lg = bk(AC).rearrange("p (t e) -> p t e", e=E)
                dve.wait_ge(s_lg, 1)
                link(dve.reduce_max(rmax[:], lg, AX.X), s_rch, rch)
                dve.tensor_tensor(rep[:], lg, rmax[:].unsqueeze(2).broadcast_to([P, NT, E]), ALU.subtract
                                  ).then_inc(s_rsh, 1)
                dve.wait_ge(s_rexp, 1)
                link(dve.reduce_sum(rsum[:], prob[:], AX.X), s_rch, rch)
                link(dve.reciprocal(rrec[:], rsum[:]), s_rch, rch)
                link(dve.tensor_tensor(prob[:], prob[:], rrec[:].unsqueeze(2).broadcast_to([P, NT, E]), ALU.mult),
                     s_rch, rch)
                for t in range(NT):
                    ins = dve.max(top[:, t, :], prob[:, t, :])
                link(ins, s_rch, rch)
                for t in range(NT):
                    dve.max_index(topi[:, t, :], top[:, t, :], prob[:, t, :])
                    ins = dve.match_replace(rep[:, t, :], top[:, t, :], prob[:, t, :], -1.0)
                link(ins, s_rch, rch)
                dve.tensor_scalar(chosen[:], rep[:], 0.0, None, ALU.is_lt).then_inc(s_chosen, 1)
                link(dve.tensor_copy(topf[:], topi[:]), s_rch, rch)

            def positions():
                pos = bk(AC).rearrange("p (t e) -> p t e", e=E)
                dve.wait_ge(s_pos, 1)
                link(dve.tensor_scalar(dest[:], pos, float(CAP), float(NOWHERE), ALU.is_ge, ALU.mult), s_rch, rch)
                link(dve.tensor_tensor(dest[:], pos, dest[:], ALU.add), s_rch, rch)
                link(dve.tensor_tensor(dest[:], dest[:], e_base[:].unsqueeze(1).broadcast_to([P, NT, E]), ALU.add),
                     s_rch, rch)

            def destination(k):
                if k == TOPK:
                    dve.tensor_copy(desti[:], destk[:]).then_inc(s_dest, 1)
                    link(dve.scalar_tensor_tensor(wts[:], destk[:], float(NOWHERE), top[:], ALU.is_lt, ALU.mult),
                         s_rch, rch)
                    return
                link(dve.tensor_tensor(rep[:], e_idx[:].unsqueeze(1).broadcast_to([P, NT, E]),
                                       topf[:, :, k:k + 1].broadcast_to([P, NT, E]), ALU.is_equal), s_rch, rch)
                link(dve.tensor_tensor(rep[:], rep[:], dest[:], ALU.mult), s_rch, rch)
                link(dve.reduce_sum(destk[:, :, k], rep[:], AX.X), s_rch, rch)

            def combine(b, i):
                t, k = JT * b + i // TOPK, i % TOPK
                if k == 0:
                    dve.wait_ge(s_yg[t % 2], 16 * TOPK * (t // 2 + 1))
                if TOPK * t + k > 0:
                    dve.wait_ge(s_comb, TOPK * t + k)
                dve.scalar_tensor_tensor(x[:, t, :], yg[t % 2][:, k, :], wts[:, t, k:k + 1], x[:, t, :],
                                         ALU.mult, ALU.add).then_inc(s_comb, 1)

            def norm(L, b):
                dve.wait_ge(s_comb, TOPK * JT * (b + 1))
                moments(L, b)
                normalise(L, b)

            def ffn_hidden(m):
                dve.wait_ge(s_fsg, m + 1)
                if m >= 2:
                    dve.wait_ge(s_fdn, m - 1)
                th = sg[m % 2][:]
                dve.scalar_tensor_tensor(th, th, 1.0, bk(GU[m % 2], 0, T), ALU.add, ALU.mult).then_inc(s_ft, 1)
                dve.wait_ge(s_ft, m + 1)
                dve.scalar_tensor_tensor(hh[m % 2][:], th, 0.5, bk(GU[m % 2], T, 2 * T), ALU.mult, ALU.mult
                                         ).then_inc(s_fh, 1)

            def ffn_add(b):
                dve.wait_ge(s_fdn, HC * (b + 1))
                dve.tensor_tensor(x[:, tiles(b), :], bk(AC).rearrange("p (j d) -> p j d", j=JT), x[:, tiles(b), :],
                                  ALU.add).then_inc(s_fadd, 1)

            def layer(L):
                for what, b, i in schedule(L):
                    g = B * L + b
                    if what == "part_hi":
                        part_rest(L, g, i)
                    if what == "part_lo":
                        part_lo(g, i)
                    if what == "router":
                        router()
                        positions()
                    if what == "destination":
                        destination(i)
                    if what == "max":
                        reduce_unit(L, g, i)
                    if what == "negate":
                        negate(L, g)
                    if what == "turn_max":
                        split_maxima(L, g)
                    if what == "hidden_sum":
                        hidden_sum(L, g, i)
                    if what == "pv0" and i == 7:
                        attended(L, g, 0)
                    if what == "pv1" and i == 3:
                        attended(L, g, 1)
                    if what == "out_proj":
                        output(L, b, g)
                    if what == "ffn_hidden":
                        ffn_hidden(i)
                    if what == "ffn_down" and i % HC == HC - 1:
                        ffn_add(b)
                    if what == "combine":
                        combine(b, i)
                    if what == "norm":
                        norm(L, b)

            for b in range(B):
                dve.wait_ge(s_x[b], 16)
                moments(0, b)
            for b in range(B):
                normalise(0, b)
            for n in range(2):
                dve.memset(ks[n][KS:KM, :, :], 1.0).then_inc(s_set, 1)
            dve.memset(nm[:], 0.0).then_inc(s_set, 1)
            dve.memset(v1[:, :, DH:V1], 1.0).then_inc(s_set, 1)
            for n in range(RING):
                dve.memset(xg[n], 0.0).then_inc(s_set, 1)
            dve.wait_ge(s_const, CONSTS)
            dve.wait_ge(s_set, SETS)
            layer(0)

            dve.wait_ge(s_tab, 16)
            dve.tensor_copy(tab_f[:], tab_i[:]).then_inc(s_tabf, 1)
            dve.wait_ge(s_tabT, 1)
            dve.tensor_copy(slots[:], bk(AC, 0, P)).then_inc(s_slots, 1)

            def rows_T(e, j):
                dve.wait_ge(s_xTp, e + BASE + 1)
                dve.wait_ge(s_gu, e + BASE + 1 - 2)
                dve.tensor_copy(xT[j % 2][:], bk(EXT[j % 2]).rearrange("p (c k) -> p c k", c=DC)).then_inc(s_xT, 1)

            def hidden(e, j):
                dve.wait_ge(s_sg, e + BASE + 1)
                dve.wait_ge(s_yp, e + BASE + 1 - 2)
                dve.tensor_tensor(hh[j % 2][0:F, :], bank[0:F, EGU[j % 2], CAP:2 * CAP], sg[j % 2][0:F, :], ALU.mult
                                  ).then_inc(s_h, 1)

            dve.sem_inc(s_xT, BASE)
            dve.sem_inc(s_h, BASE)
            rows_T(0, 0)
            rows_T(1, 1)
            hidden(0, 0)
            with dve.Fori(0, E // RING - 1) as i:
                for j in range(RING):
                    e = i * RING + j
                    rows_T(e + 2, (j + 2) % RING)
                    hidden(e + 1, (j + 1) % RING)
            for e in range(E - RING, E):
                if e + 2 < E:
                    rows_T(e + 2, (e + 2) % RING)
                if e + 1 < E:
                    hidden(e + 1, (e + 1) % RING)

            for i in range(JT * TOPK):
                combine(0, i)
            norm(1, 0)
            layer(1)


_OUT = ((B, T, D), "float32")


def kernel(**inputs):
    import numpy as np
    import concourse.bacc as bacc
    from concourse.bass_utils import run_bass_kernel_spmd

    a = {name: np.asarray(v) for name, v in inputs.items()}

    def expert_in(w):
        return np.ascontiguousarray(w.transpose(0, 2, 1).reshape(E, DC, P, F).transpose(0, 2, 1, 3))

    def by_channel(w):
        return w.reshape(D, H, DH).transpose(0, 2, 1).reshape(D, D)

    laid = {
        "x_in": a["L0_attn_x"],
        "wq0": by_channel(a["L0_attn_Wq"]), "wk0": by_channel(a["L0_attn_Wk"]), "wv0": a["L0_attn_Wv"], "wo0": a["L0_attn_Wo"],
        "gate_w": a["L0_ffn_gate_w"].T,
        "e_gate": expert_in(a["L0_ffn_w_gate"]), "e_up": expert_in(a["L0_ffn_w_up"]),
        "e_down": a["L0_ffn_w_down"].transpose(0, 2, 1),
        "wq1": by_channel(a["L1_attn_Wq"].T), "wk1": by_channel(a["L1_attn_Wk"].T), "wv1": a["L1_attn_Wv"].T, "wo1": a["L1_attn_Wo"].T,
        "f_gate": a["L1_ffn_w_gate"].T, "f_up": a["L1_ffn_w_up"].T, "f_down": a["L1_ffn_w_down"].T,
    }
    nc = bacc.Bacc("TRN2", target_bir_lowering=False, num_devices=1)
    arrays, args = {}, []
    for name, v in laid.items():
        v = np.ascontiguousarray(v)
        arrays[name] = v
        args.append(nc.dram_tensor(name, v.shape, mybir.dt.from_np(v.dtype), kind="ExternalInput").ap())
    shape, dtype = _OUT
    args.append(nc.dram_tensor("out", shape, mybir.dt.from_np(np.dtype(dtype)), kind="ExternalOutput").ap())
    build(nc, *args)
    return run_bass_kernel_spmd(nc, [arrays], core_ids=[0]).results[0]["out"]
```
